# Optimizing a Trainium2 kernel written in Bass

```python
import numpy as np
import jax
import jax.numpy as jnp

def _softmax(x, axis=-1):
    return jax.nn.softmax(x, axis=axis)

def _gelu(x):
    return jax.nn.gelu(x, approximate=True)

def _silu(x):
    return jax.nn.silu(x)

def _sigmoid(x):
    return jax.nn.sigmoid(x)

def _layernorm(x, axis=-1, eps=1e-05):
    m = jnp.mean(x, axis=axis, keepdims=True)
    v = jnp.var(x, axis=axis, keepdims=True)
    return (x - m) / jnp.sqrt(v + eps)

def _scatter_add(tgt, idx, src, axis=0):
    return tgt.at[idx].add(src)

def _segment_sum(src, seg, n):
    return jax.ops.segment_sum(src, seg, n)
kernel_name = 'mk_conv_preact_d1_conv_nchw256_r4_c3fd2f'

def setup_inputs(seed: int=0):
    np.random.seed(seed)
    _w = jnp.asarray

    def _rec_inputs():
        import jax
        import jax.numpy as jnp
        _gk = jax.random.key(seed)
        x = -0.0001732 + 1 * jax.random.normal(jax.random.fold_in(_gk, 1), (8, 64, 48, 48), jnp.float32)
        return x
    x = _rec_inputs()

    def _L0_conv_setup():
        import jax, jax.numpy as jnp
        import numpy as np
        B, IN_C, OUT_C, K, S, H, W = (8, 64, 64, 3, 8, 48, 48)
        key = jax.random.key(seed)
        k1, k2, k3, k4, k5 = jax.random.split(key, 5)
        fan_in = IN_C * K * K
        return {'x': jax.random.normal(k1, (B, IN_C, H, W), jnp.float32), 'coupler_w': jax.random.normal(k2, (S, IN_C, 1, 1), jnp.float32) * 0.05, 'coupler_b': jax.random.normal(k3, (S,), jnp.float32) * 0.05, 'weight': jax.random.normal(k4, (OUT_C, IN_C, S, K, K), jnp.float32) * (1.0 / np.sqrt(fan_in)), 'bias': jax.random.normal(k5, (OUT_C,), jnp.float32) * 0.05}
    _L0_conv_all = _L0_conv_setup()
    _L0_conv_in = {k: v for k, v in _L0_conv_all.items() if k in ('coupler_w', 'coupler_b', 'weight', 'bias')}
    del _L0_conv_all
    return {'x': x, 'L0_conv_coupler_w': _L0_conv_in['coupler_w'], 'L0_conv_coupler_b': _L0_conv_in['coupler_b'], 'L0_conv_weight': _L0_conv_in['weight'], 'L0_conv_bias': _L0_conv_in['bias']}

def reference(x, L0_conv_coupler_w, L0_conv_coupler_b, L0_conv_weight, L0_conv_bias):
    import jax
    import jax.numpy as jnp

    def _L0_conv_ref(x, coupler_w, coupler_b, weight, bias):
        import jax, jax.numpy as jnp
        import numpy as np
        B, IN_C, OUT_C, K, S, H, W = (8, 64, 64, 3, 8, 48, 48)
        dn1 = jax.lax.conv_dimension_numbers(x.shape, coupler_w.shape, ('NCHW', 'OIHW', 'NCHW'))
        logits = jax.lax.conv_general_dilated(x, coupler_w, (1, 1), 'VALID', dimension_numbers=dn1)
        logits = logits + coupler_b[None, :, None, None]
        sel = jax.nn.softmax(logits, axis=1)
        sel = sel / sel.sum(axis=1, keepdims=True)
        oc, ic, s, k = (weight.shape[0], weight.shape[1], weight.shape[2], weight.shape[3])
        w = jnp.transpose(weight, (2, 0, 1, 3, 4)).reshape(s * oc, ic, k, k)
        pad = k // 2
        dn2 = jax.lax.conv_dimension_numbers(x.shape, w.shape, ('NCHW', 'OIHW', 'NCHW'))
        conv = jax.lax.conv_general_dilated(x, w, (1, 1), [(pad, pad), (pad, pad)], dimension_numbers=dn2)
        b_, _, h_, w_ = conv.shape
        conv = conv.reshape(b_, s, oc, h_, w_) + bias[None, None, :, None, None]
        return jnp.einsum('bschw,bshw->bchw', conv, sel)

    def _gn(v, G=32, eps=1e-05):
        B_, C_, H_, W_ = v.shape
        g = v.reshape(B_, G, C_ // G, H_, W_)
        m = jnp.mean(g, axis=(2, 3, 4), keepdims=True)
        s = jnp.var(g, axis=(2, 3, 4), keepdims=True)
        return ((g - m) / jnp.sqrt(s + eps)).reshape(v.shape)

    def _ln_c(v, eps=1e-06):
        m = jnp.mean(v, axis=1, keepdims=True)
        s = jnp.var(v, axis=1, keepdims=True)
        return (v - m) / jnp.sqrt(s + eps)

    def _ln_t(v, eps=1e-05):
        m = jnp.mean(v, axis=-1, keepdims=True)
        s = jnp.var(v, axis=-1, keepdims=True)
        return (v - m) / jnp.sqrt(s + eps)

    def _to_tokens(v):
        B_, C_, H_, W_ = v.shape
        return v.reshape(B_, C_, H_ * W_).transpose(0, 2, 1)

    def _from_tokens(t, like):
        B_, C_, H_, W_ = like.shape
        return t.transpose(0, 2, 1).reshape(B_, C_, H_, W_)
    x = x + _L0_conv_ref(_gn(x), L0_conv_coupler_w, L0_conv_coupler_b, L0_conv_weight, L0_conv_bias)
    return x

_drawn_inputs = setup_inputs


def setup_inputs(seed=0):
    import zlib

    import numpy as np

    out = dict(_drawn_inputs(seed))
    spreads = {}
    factors = {'L0_conv_coupler_b': 3.982}
    for name, (base, spread) in spreads.items():
        noise = np.random.default_rng([zlib.crc32(name.encode()), seed]).standard_normal(out[name].shape)
        drawn = base * np.exp(spread * noise) if base else spread * noise
        out[name] = jnp.asarray(drawn.astype(out[name].dtype))
    for name, factor in factors.items():
        out[name] = (out[name] * factor).astype(out[name].dtype)
    return out
```

```python
from contextlib import ExitStack

from concourse import mybir

F32 = mybir.dt.float32
F16 = mybir.dt.float16
I32 = mybir.dt.int32
ALU = mybir.AluOpType
ACT = mybir.ActivationFunctionType
AX = mybir.AxisListType

P = 128
IMAGES, C, H, W = 8, 64, 48, 48
SETS, K = 8, 3
HW = H * W
ROUNDS = IMAGES // 2
PW = W // 2
PAIRS = H * PW
TPI = PAIRS // P
TILES = 2 * TPI
PADDED = (H + 2) * PW
N = SETS * C
POINTS = (1, 2, 0, 3)
NP = len(POINTS)
CHUNK = 384
CHUNKS = HW // CHUNK
EPS = 1e-5
X_SCALE = 512.0
W_TOP = 2.0 ** 14
TINY = 2.0 ** -100
PIX = 2 * TILES
LOOK = 2
SETS_OF_BANKS = 3

PREP_CHAIN = 16
F_PARTS = 4


def program(nc, x, x_pix, weight, bias, coupler_w, coupler_b, matrices, out):
    with ExitStack() as ctx:
        def sb(name, shape, dt=F32):
            return ctx.enter_context(nc.sbuf_tensor(name, shape, dt))

        def sem(name):
            return ctx.enter_context(nc.semaphore(name))

        w_raw = sb("w_raw", [P, K, K, N])
        w_sum = sb("w_sum", [P, K, N])
        w_pts = sb("w_pts", [P, 2, K, N])
        w_head = sb("w_head", [P, NP, K, N], F16)
        w_tail01 = sb("w_tail01", [P, NP, N], F16)
        w_tail2 = sb("w_tail2", [P, NP, N], F16)
        w_max = sb("w_max", [P, 2])
        w_top = sb("w_top", [P, 1])
        w_scale = sb("w_scale", [P, 4])
        ones = sb("ones", [1, P])
        cw_pair = sb("cw_pair", [P, 2, SETS])
        cb_all = sb("cb_all", [P, SETS])
        bias_all = sb("bias_all", [P, C])
        mats = sb("mats", [P, 3, P])
        mean_mat, diff_mat, ident = (mats[:, k, :] for k in range(3))
        minus_half = sb("minus_half", [P, 1])

        x_raw = sb("x_raw", [P, HW])
        x_norm = sb("x_norm", [P, HW])
        stats = sb("stats", [P, CHUNKS, 6])
        mean_var = sb("mean_var", [P, 2])
        group = sb("group", [P, 3])
        diff_sq = sb("diff_sq", [P, 1])
        var_eps = sb("var_eps", [P, 1])
        rstd = sb("rstd", [P, 1])
        norm_scale = sb("norm_scale", [P, 1])
        v_pts = sb("v_pts", [P, NP, PAIRS])
        v_head = sb("v_head", [P, NP, PADDED], F16)
        v_tail = sb("v_tail", [P, NP, PADDED], F16)
        logit = sb("logit", [P, PIX, SETS])
        top = sb("top", [P, PIX])
        total = sb("total", [P, PIX])
        mix = sb("mix", [P, PIX, SETS])
        sel_next = sb("sel_next", [P, PIX * (SETS + 1)])
        sel_now = sb("sel_now", [P, PIX * (SETS + 1)])

        op_ht = [sb(f"op_ht{b}", [P, NP, PADDED], F16) for b in range(2)]
        op_hh = [sb(f"op_hh{b}", [P, NP, PAIRS], F16) for b in range(2)]

        m1_sb = sb("m1_sb", [P, LOOK, N])
        prod = sb("prod", [P, LOOK, 2, SETS, C])
        half = sb("half", [P, LOOK, 2, SETS // 2, C])
        quarter = sb("quarter", [P, 2, SETS // 4, C])
        mixed = sb("mixed", [P, 2, C])
        x_res = [sb(f"x_res{b}", [P, TPI, 2, C]) for b in range(2)]
        bias_part = sb("bias_part", [P, TPI * 2, C])
        y_out = [sb(f"y_out{b}", [P, TPI, 2, C]) for b in range(2)]

        bank = [ctx.enter_context(nc.psum_tensor(f"bank{b}", [P, N], F32)) for b in range(2 * SETS_OF_BANKS)]
        side = ctx.enter_context(nc.psum_tensor("side", [P, N], F32))
        w_bank = ctx.enter_context(nc.psum_tensor("w_bank", [P, N], F32))
        logit_ps = side[:, 0:PIX * SETS]
        group_ps = side[:, PIX * SETS:PIX * SETS + 3]

        small_loaded = sem("small_loaded")
        w_loaded = sem("w_loaded")
        ready = sem("ready")
        cleared = sem("cleared")
        w_chain = sem("w_chain")
        w_col = sem("w_col")
        w_cast = sem("w_cast")
        w_sums = sem("w_sums")
        w_heads = sem("w_heads")
        w_tails = sem("w_tails")

        x_loaded = sem("x_loaded")
        prep = sem("prep")
        group_done = sem("group_done")
        rstd_done = sem("rstd_done")
        norm_done = sem("norm_done")
        v_done = sem("v_done")
        edge_done = sem("edge_done")
        h_done = sem("h_done")
        t_done = sem("t_done")
        logit_done = sem("logit_done")
        exp_done = sem("exp_done")
        sel_done = sem("sel_done")
        sel_copied = sem("sel_copied")
        ops_in = [[sem(f"ops_in{b}_{g}") for g in range(2)] for b in range(2)]

        m1_done = sem("m1_done")
        m2_done = sem("m2_done")
        m1_copied = sem("m1_copied")
        seeded = sem("seeded")
        y_done = sem("y_done")
        prod_done = sem("prod_done")
        half_done = sem("half_done")
        half_used = sem("half_used")
        mixed_done = sem("mixed_done")
        out_done = sem("out_done")
        xres_in = [sem(f"xres_in{b}") for b in range(2)]
        bias_done = sem("bias_done")
        xb_done = sem("xb_done")
        stored = [sem(f"stored{b}") for b in range(2)]

        x_pair = x.rearrange("(n b) c h w -> n (b c) (h w)", b=2)
        x_pix_v = x_pix.rearrange("(n b) t p k -> n b p t k", b=2)
        out_v = out.rearrange("(n b) t p k -> n b p t k", b=2)

        sel_w = sel_now[:, 0:PIX * SETS].rearrange("p (q s) -> p q s", s=SETS)
        sel_sum = sel_now[:, PIX * SETS:PIX * (SETS + 1)]
        sel_next_w = sel_next[:, 0:PIX * SETS].rearrange("p (q s) -> p q s", s=SETS)
        sel_next_sum = sel_next[:, PIX * SETS:PIX * (SETS + 1)]

        def spread(ap, n):
            return ap.unsqueeze(2).to_broadcast([P, ap.shape[1], n])

        block = ctx.enter_context(nc.Block())

        @block.sync
        def _(sp):
            def wait(signal, value):
                sp.wait_ge(signal, value)
                sp.nop(nofuse=True)

            def load_pair(m):
                sp.dma_start(x_raw[:, :], x_pair[m, :, :]).then_inc(x_loaded, 16)

            def fill_ops(b, g, m):
                wait(t_done, m * NP + 2 * g + 2)
                lo, pts = C * b, slice(2 * g, 2 * g + 2)
                here = v_head[lo:lo + C, pts, :]
                sp.dma_start(op_ht[b][0:C, pts, :], here).then_inc(ops_in[b][g], 16)
                sp.dma_start(op_ht[b][C:P, pts, :], v_tail[lo:lo + C, pts, :]).then_inc(ops_in[b][g], 16)
                sp.dma_start(op_hh[b][0:C, pts, :], here[:, :, 0:PAIRS]).then_inc(ops_in[b][g], 16)
                sp.dma_start(op_hh[b][C:P, pts, :], here[:, :, PW:PW + PAIRS]).then_inc(ops_in[b][g], 16)

            def load_res(b, n):
                sp.dma_start(x_res[b].rearrange("p t a c -> p t (a c)"), x_pix_v[n, b, :, :, :]).then_inc(xres_in[b], 16)

            def store(b, n, t0, t1):
                wait(out_done, n * TILES + b * TPI + t1 + 1)
                sp.dma_start(out_v[n, b, :, t0:t1, :],
                             y_out[b][:, t0:t1, :, :].rearrange("p t a c -> p t (a c)")).then_inc(stored[b], 16)

            load_pair(0)
            for half_p in range(2):
                sp.dma_start(w_raw[C * half_p:C * half_p + C, :, :, :].rearrange("p a b n -> p (a b n)"),
                             weight).then_inc(w_loaded, 16)
            sp.dma_start(mats[:, :, :], matrices).then_inc(small_loaded, 16)
            sp.dma_start(bias_all[:, :], bias.partition_broadcast(P)).then_inc(small_loaded, 16)
            sp.dma_start(cb_all[:, :], coupler_b.partition_broadcast(P)).then_inc(small_loaded, 16)
            wait(cleared, 1)
            for b in range(2):
                sp.dma_start(cw_pair[C * b:C * b + C, b, :], coupler_w).then_inc(small_loaded, 16)
            fill_ops(0, 0, 0)
            fill_ops(0, 1, 0)
            load_res(0, 0)

            def round_(n, more):
                if more:
                    wait(norm_done, n + 1)
                    load_pair(n + 1)
                wait(prod_done, n * 2 * TILES + 2 * SETS_OF_BANKS)
                fill_ops(1, 0, n)
                fill_ops(1, 1, n)
                wait(out_done, n * TILES + 1)
                load_res(1, n)
                store(0, n, 0, TPI)
                if more:
                    load_res(0, n + 1)
                    wait(prod_done, n * 2 * TILES + 2 * TPI + 2 * SETS_OF_BANKS)
                    fill_ops(0, 0, n + 1)
                    fill_ops(0, 1, n + 1)
                    store(1, n, 0, TPI)
                else:
                    store(1, n, 0, TPI - 2)
                    store(1, n, TPI - 2, TPI - 1)
                    store(1, n, TPI - 1, TPI)

            with sp.Fori(0, ROUNDS - 1) as n:
                round_(n, True)
            round_(ROUNDS - 1, False)
            wait(stored[0], 16 * (ROUNDS + 1))
            wait(stored[1], 16 * (ROUNDS + 3))

        @block.tensor
        def _(pe):
            def group_sums(m):
                if not isinstance(m, int) or m:
                    pe.wait_ge(prep, m * PREP_CHAIN)
                pe.wait_ge(prep, m * PREP_CHAIN + 2)
                nc.tensor.matmul(group_ps[:, 0:2], mean_mat[:, :], mean_var[:, :], start=True, stop=True)
                nc.tensor.matmul(group_ps[:, 2:3], diff_mat[:, :], mean_var[:, 0:1], start=True, stop=True) \
                    .then_inc(group_done, 1)

            def logits(m):
                pe.wait_ge(norm_done, m + 1)
                lg = logit_ps.rearrange("p (b t a s) -> p t a b s", b=2, t=TPI, a=2)
                xv = x_norm[:, :].rearrange("p (t q a) -> p t a q", t=TPI, a=2)
                for t in range(TPI):
                    for a in range(2):
                        last = nc.tensor.matmul(lg[:, t, a, :, :], xv[:, t, a, :], cw_pair[:, :, :], start=True, stop=True)
                last.then_inc(logit_done, 1)

            def point(b, j, t, dst, fresh):
                at = t * P
                for r in range(K):
                    nc.tensor.matmul(dst, op_ht[b][:, j, at + r * PW:at + r * PW + P], w_head[:, j, r, :],
                                     start=fresh and r == 0, stop=False, skip_group_check=True)
                nc.tensor.matmul(dst, op_ht[b][:, j, at + 2 * PW:at + 2 * PW + P], w_tail2[:, j, :],
                                 start=False, stop=False, skip_group_check=True)
                return nc.tensor.matmul(dst, op_hh[b][:, j, at:at + P], w_tail01[:, j, :],
                                        start=False, stop=True, skip_group_check=True)

            def first_points(i, n):
                b, t, s = i // TPI, i % TPI, i % SETS_OF_BANKS
                if t == 0:
                    pe.wait_ge(ops_in[b][0], (n + 1) * 16 * F_PARTS)
                for a in range(2):
                    pe.wait_ge(prod_done, n * 2 * TILES + 2 * i + a + 1)
                    point(b, a, t, bank[2 * s + a][:, :], True).then_inc((m1_done, m2_done)[a], 1)

            def last_points(i, n):
                b, t, s = i // TPI, i % TPI, i % SETS_OF_BANKS
                if t == 0:
                    pe.wait_ge(ops_in[b][1], (n + 1) * 16 * F_PARTS)
                for a in range(2):
                    pe.wait_ge(seeded, n * 2 * TILES + 2 * i + a + 1 + 2 * LOOK)
                    point(b, 2 + a, t, bank[2 * s + a][:, :], False).then_inc(y_done, 1)

            def round_(n, more):
                for i in range(TILES):
                    first_points(i, n)
                    if i:
                        last_points(i - 1, n)
                    if more and i == 3:
                        group_sums(n + 1)
                    if more and i == 9:
                        logits(n + 1)
                last_points(TILES - 1, n)

            pe.wait_ge(small_loaded, 16 * 5)
            group_sums(0)
            logits(0)
            pe.wait_ge(ready, 1)
            pe.wait_ge(w_chain, 3)
            nc.tensor.matmul(w_bank[0:1, 0:P], w_max[:, 1:2], ident[:, :], start=True, stop=True).then_inc(w_col, 1)
            pe.wait_ge(w_chain, 4)
            nc.tensor.matmul(w_bank[:, P:P + 1], ones[0:1, :], w_top[0:1, 0:1], start=True, stop=True).then_inc(w_cast, 1)
            pe.wait_ge(w_tails, NP)
            with pe.Fori(0, ROUNDS - 1) as n:
                round_(n, True)
            round_(ROUNDS - 1, False)

        @block.scalar
        def _(act):
            def input_heads(m, k, first=False):
                act.wait_ge(v_done, m * NP + k + 1)
                if k >= 2:
                    v_rows = v_pts[:, k, :].rearrange("p (h w) -> p h w", w=PW)
                    x_rows = x_norm[:, :].rearrange("p (h w a) -> p h w a", w=PW, a=2)
                    col, a = ((0, 1), (PW - 1, 0))[k - 2]
                    act.activation(v_rows[:, :, col:col + 1], x_rows[:, :, col:col + 1, a], ACT.Copy, scale=-1.0) \
                        .then_inc(edge_done, 1)
                    act.wait_ge(edge_done, m * 2 + k - 1)
                if not first:
                    for b in range(2):
                        act.wait_ge(ops_in[b][k // 2], m * 16 * F_PARTS)
                act.activation(v_head[:, k, PW:PW + PAIRS], v_pts[:, k, :], ACT.Copy).then_inc(h_done, 1)

            def exponentials(m):
                act.wait_ge(prep, m * PREP_CHAIN + 9)
                act.activation(mix[:, :, :], logit[:, :, :], ACT.Exp).then_inc(exp_done, 1)

            def round_(n, more):
                for i in range(TILES):
                    act.wait_ge(m1_done, n * TILES + i + 1)
                    act.wait_ge(seeded, n * 2 * TILES + 2 * i + 2)
                    act.activation(m1_sb[:, i % LOOK, :], bank[2 * (i % SETS_OF_BANKS)][:, :], ACT.Copy) \
                        .then_inc(m1_copied, 1)
                    if more and 9 <= i < 9 + NP:
                        input_heads(n + 1, i - 9)
                    if more and i == 13:
                        exponentials(n + 1)

            act.wait_ge(ready, 1)
            for k in range(NP):
                input_heads(0, k, True)
            for k in range(NP):
                act.wait_ge(w_chain, 9)
                if k < 2:
                    act.wait_ge(w_sums, k + 2)
                src = w_pts[:, k, :, :] if k < 2 else w_raw[:, :, 2 * (k - 2), :]
                act.activation(w_head[:, k, :, :], src, ACT.Copy,
                               scale=w_scale[:, 2:3] if k < 2 else w_scale[:, 1:2]).then_inc(w_heads, 1)
            exponentials(0)
            with act.Fori(0, ROUNDS - 1) as n:
                round_(n, True)
            round_(ROUNDS - 1, False)

        @block.vector
        def _(dve):
            def statistics(m):
                dve.wait_ge(x_loaded, (m + 1) * 16)
                for k in range(CHUNKS):
                    last = dve.bn_stats(stats[:, k, :], x_raw[:, k * CHUNK:(k + 1) * CHUNK])
                last.then_inc(prep, 1)

            def aggregate(m):
                dve.wait_ge(prep, m * PREP_CHAIN + 1)
                dve.nop(nofuse=True)
                dve.bn_aggr(mean_var[:, :], stats[:, :, :]).then_inc(prep, 1)

            def group_variance(m):
                dve.wait_ge(group_done, m + 1)
                dve.tensor_copy(group[:, :], group_ps).then_inc(prep, 1)
                dve.wait_ge(prep, m * PREP_CHAIN + 3)
                dve.tensor_tensor(diff_sq[:, :], group[:, 2:3], group[:, 2:3], ALU.mult).then_inc(prep, 1)
                dve.wait_ge(prep, m * PREP_CHAIN + 4)
                dve.scalar_tensor_tensor(var_eps[:, :], group[:, 1:2], EPS, diff_sq[:, :], ALU.add, ALU.add).then_inc(prep, 1)

            def normalise(m, first=False):
                dve.wait_ge(rstd_done, m + 1)
                dve.tensor_scalar(norm_scale[:, :], rstd[:, :], X_SCALE, None, ALU.mult).then_inc(prep, 1)
                dve.wait_ge(prep, m * PREP_CHAIN + 6)
                if not first:
                    dve.wait_ge(logit_done, m)
                    dve.wait_ge(edge_done, m * 2)
                dve.tensor_scalar(x_norm[:, :], x_raw[:, :], group[:, 0:1], norm_scale[:, 0:1],
                                  ALU.subtract, ALU.mult).then_inc(norm_done, 1)

            def input_point(m, k, first=False):
                dve.wait_ge(norm_done, m + 1)
                if not first:
                    dve.wait_ge(t_done, m * NP - NP + k + 1)
                even, odd = (x_norm[:, :].rearrange("p (q a) -> p q a", a=2)[:, :, a] for a in range(2))
                e_rows, o_rows = (v.rearrange("p (h w) -> p h w", w=PW) for v in (even, odd))
                v = v_pts[:, k, :]
                v_rows = v.rearrange("p (h w) -> p h w", w=PW)
                if k == 0:
                    ins = dve.tensor_tensor(v, even, odd, ALU.add)
                elif k == 1:
                    ins = dve.tensor_tensor(v, odd, even, ALU.subtract)
                elif k == 2:
                    ins = dve.tensor_tensor(v_rows[:, :, 1:PW], o_rows[:, :, 0:PW - 1], o_rows[:, :, 1:PW], ALU.subtract)
                else:
                    ins = dve.tensor_tensor(v_rows[:, :, 0:PW - 1], e_rows[:, :, 1:PW], e_rows[:, :, 0:PW - 1], ALU.subtract)
                ins.then_inc(v_done, 1)

            def softmax_in(m):
                dve.wait_ge(logit_done, m + 1)
                dve.scalar_tensor_tensor(logit[:, :, :], logit_ps.rearrange("p (q s) -> p q s", s=SETS), 1.0 / X_SCALE,
                                         cb_all[:, :].unsqueeze(1).to_broadcast([P, PIX, SETS]), ALU.mult, ALU.add) \
                    .then_inc(prep, 1)
                dve.wait_ge(prep, m * PREP_CHAIN + 7)
                dve.tensor_reduce(top[:, :], logit[:, :, :], axis=AX.X, op=ALU.max).then_inc(prep, 1)
                dve.wait_ge(prep, m * PREP_CHAIN + 8)
                dve.tensor_tensor(logit[:, :, :], logit[:, :, :], spread(top[:, :], SETS), ALU.subtract).then_inc(prep, 1)

            def softmax_out(m):
                dve.wait_ge(exp_done, m + 1)
                dve.tensor_reduce(total[:, :], mix[:, :, :], axis=AX.X, op=ALU.add).then_inc(prep, 1)
                dve.wait_ge(prep, m * PREP_CHAIN + 10)
                dve.reciprocal(total[:, :], total[:, :]).then_inc(prep, 1)
                dve.wait_ge(prep, m * PREP_CHAIN + 11)
                dve.tensor_tensor(logit[:, :, :], mix[:, :, :], spread(total[:, :], SETS), ALU.mult).then_inc(prep, 1)
                dve.wait_ge(prep, m * PREP_CHAIN + 12)
                dve.tensor_reduce(top[:, :], logit[:, :, :], axis=AX.X, op=ALU.add).then_inc(prep, 1)
                dve.wait_ge(prep, m * PREP_CHAIN + 13)
                dve.reciprocal(top[:, :], top[:, :]).then_inc(prep, 1)
                dve.wait_ge(prep, m * PREP_CHAIN + 14)
                dve.tensor_tensor(mix[:, :, :], logit[:, :, :], spread(top[:, :], SETS), ALU.mult).then_inc(prep, 1)
                dve.wait_ge(prep, m * PREP_CHAIN + 15)
                dve.tensor_reduce(sel_next_sum, mix[:, :, :], axis=AX.X, op=ALU.add).then_inc(prep, 1)
                dve.tensor_scalar(sel_next_w, mix[:, :, :], w_scale[:, 3:4], None, ALU.mult).then_inc(sel_done, 1)

            def seed(i, n):
                plus, minus = (bank[2 * (i % SETS_OF_BANKS) + a] for a in range(2))
                m1 = m1_sb[:, i % LOOK, :]
                dve.wait_ge(m2_done, n * TILES + i + 1)
                dve.wait_ge(m1_copied, n * TILES + i + 1)
                dve.tensor_tensor(plus[:, :], minus[:, :], m1, ALU.add).then_inc(seeded, 1)
                dve.tensor_tensor(minus[:, :], m1, minus[:, :], ALU.subtract).then_inc(seeded, 1)

            def multiply(i, n):
                dve.wait_ge(half_done, n * TILES + i + 1)
                for a in range(2):
                    dve.wait_ge(y_done, n * 2 * TILES + 2 * i + a + 1)
                    dve.tensor_tensor(prod[:, i % LOOK, a, :, :],
                                      bank[2 * (i % SETS_OF_BANKS) + a][:, :].rearrange("p (s c) -> p s c", c=C),
                                      spread(sel_w[:, 2 * i + a, :], C), ALU.mult).then_inc(prod_done, 1)

            def halve(i, n):
                dve.wait_ge(prod_done, n * 2 * TILES + 2 * i + 2 + 2 * SETS_OF_BANKS)
                dve.wait_ge(half_used, n * TILES + i + 1)
                p4 = prod[:, i % LOOK, :, :, :]
                dve.tensor_tensor(half[:, i % LOOK, :, :, :].rearrange("p a s c -> p a (s c)"),
                                  p4[:, :, 0:SETS // 2, :].rearrange("p a s c -> p a (s c)"),
                                  p4[:, :, SETS // 2:SETS, :].rearrange("p a s c -> p a (s c)"), ALU.add).then_inc(half_done, 1)

            def round_(n, more):
                dve.wait_ge(sel_done, n + 1)
                dve.wait_ge(xb_done, n * 2 + 1)
                dve.tensor_copy(sel_now[:, :], sel_next[:, :]).then_inc(sel_copied, 1)
                for i in range(TILES):
                    seed(i, n)
                    if i == 1:
                        dve.wait_ge(sel_copied, n + 1)
                    if i >= 1:
                        multiply(i - 1, n)
                    if i >= 2:
                        halve(i - 2, n)
                    if more and i == 1:
                        statistics(n + 1)
                        aggregate(n + 1)
                    if more and i == 4:
                        group_variance(n + 1)
                    if more and i == 6:
                        normalise(n + 1)
                    if more and 7 <= i < 7 + NP:
                        input_point(n + 1, i - 7)
                    if more and i == 12:
                        softmax_in(n + 1)
                    if more and i == 15:
                        softmax_out(n + 1)
                multiply(TILES - 1, n)
                halve(TILES - 2, n)
                halve(TILES - 1, n)

            dve.memset(w_top[:, :], 0.0).then_inc(seeded, 2 * LOOK)
            dve.memset(var_eps[:, :], 0.0).then_inc(prod_done, 2 * SETS_OF_BANKS)
            dve.memset(diff_sq[:, :], 0.0).then_inc(half_done, LOOK)
            statistics(0)
            aggregate(0)
            group_variance(0)
            normalise(0, True)
            for k in range(NP):
                input_point(0, k, True)
            dve.wait_ge(ready, 1)
            for k in range(NP):
                dve.wait_ge(h_done, k + 1)
                dve.tensor_tensor(v_tail[:, k, PW:PW + PAIRS], v_pts[:, k, :], v_head[:, k, PW:PW + PAIRS],
                                  ALU.subtract).then_inc(t_done, 1)
            dve.wait_ge(w_loaded, 16 * 2)
            dve.tensor_reduce(w_max[:, 0:1], w_raw[:, :, :, :].rearrange("p a b n -> p (a b n)"), axis=AX.X, op=ALU.max,
                              apply_absolute_value=True).then_inc(w_chain, 1)
            dve.wait_ge(w_chain, 1)
            dve.tensor_scalar(w_max[:, 0:1], w_max[:, 0:1], TINY, None, ALU.max).then_inc(w_chain, 1)
            dve.wait_ge(w_chain, 2)
            dve.tensor_scalar(w_max[:, 1:2].bitcast(I32), w_max[:, 0:1].bitcast(I32), 0x7F800000, None,
                              ALU.bitwise_and).then_inc(w_chain, 1)
            dve.wait_ge(w_col, 1)
            dve.tensor_reduce(w_top[0:1, :], w_bank[0:1, 0:P], axis=AX.X, op=ALU.max).then_inc(w_chain, 1)
            for r in range(K):
                last = dve.tensor_tensor(w_sum[:, r, :], w_raw[:, r, 0, :], w_raw[:, r, 2, :], ALU.add)
            last.then_inc(w_sums, 1)
            dve.wait_ge(w_sums, 1)
            dve.wait_ge(w_cast, 1)
            dve.tensor_copy(w_scale[:, 0:1], w_bank[:, P:P + 1]).then_inc(w_chain, 1)
            dve.wait_ge(w_chain, 5)
            dve.reciprocal(w_scale[:, 1:2], w_scale[:, 0:1]).then_inc(w_chain, 1)
            dve.tensor_scalar(w_scale[:, 3:4], w_scale[:, 0:1], 1.0 / (W_TOP * X_SCALE), None, ALU.mult).then_inc(w_chain, 1)
            dve.wait_ge(w_chain, 6)
            dve.tensor_scalar(w_scale[:, 2:3], w_scale[:, 1:2], W_TOP / 2, None, ALU.mult).then_inc(w_chain, 1)
            dve.tensor_scalar(w_scale[:, 1:2], w_scale[:, 1:2], W_TOP, None, ALU.mult).then_inc(w_chain, 1)
            for k, op in enumerate((ALU.add, ALU.subtract)):
                dve.tensor_tensor(w_pts[:, k, :, :], w_sum[:, :, :], w_raw[:, :, 1, :], op).then_inc(w_sums, 1)
            dve.wait_ge(w_chain, 9)
            for k in range(NP):
                dve.wait_ge(w_heads, k + 1)
                src = w_pts[:, k, :, :] if k < 2 else w_raw[:, :, 2 * (k - 2), :]
                for lo, hi, r, tail in ((0, C, 0, w_tail01), (C, P, 1, w_tail01), (0, P, 2, w_tail2)):
                    scale = w_scale[lo:hi, 2:3] if k < 2 else w_scale[lo:hi, 1:2]
                    last = dve.scalar_tensor_tensor(tail[lo:hi, k, :], src[lo:hi, r, :], scale, w_head[lo:hi, k, r, :],
                                                    ALU.mult, ALU.subtract)
                last.then_inc(w_tails, 1)
            dve.wait_ge(small_loaded, 16 * 5)
            softmax_in(0)
            softmax_out(0)
            with dve.Fori(0, ROUNDS - 1) as n:
                round_(n, True)
            round_(ROUNDS - 1, False)

        @block.gpsimd
        def _(pool):
            def inverse_deviation(m):
                pool.wait_ge(prep, m * PREP_CHAIN + 5)
                pool.tensor_tensor(rstd[:, :], var_eps[:, :], minus_half[:, :], ALU.pow).then_inc(rstd_done, 1)

            def input_tails(m, k):
                pool.wait_ge(h_done, m * NP + k + 1)
                for b in range(2):
                    pool.wait_ge(ops_in[b][k // 2], m * 16 * F_PARTS)
                pool.tensor_tensor(v_tail[:, k, PW:PW + PAIRS], v_pts[:, k, :], v_head[:, k, PW:PW + PAIRS],
                                   ALU.subtract).then_inc(t_done, 1)

            def input_and_bias(b, n):
                pool.wait_ge(sel_copied, n + 1)
                q0 = b * TPI * 2
                pool.tensor_tensor(bias_part[:, :, :], bias_all[:, :].unsqueeze(1).to_broadcast([P, TPI * 2, C]),
                                   spread(sel_sum[:, q0:q0 + TPI * 2], C), ALU.mult).then_inc(bias_done, 1)
                pool.wait_ge(xres_in[b], (n + 1) * 16)
                pool.wait_ge(bias_done, n * 2 + b + 1)
                xr = x_res[b][:, :, :, :].rearrange("p t a c -> p (t a) c")
                pool.tensor_tensor(xr, xr, bias_part[:, :, :], ALU.add).then_inc(xb_done, 1)

            def finish(i, n):
                b, t = i // TPI, i % TPI
                pool.wait_ge(half_done, n * TILES + i + 1 + LOOK)
                hf = half[:, i % LOOK, :, :, :]
                pool.tensor_tensor(quarter[:, :, :, :].rearrange("p a s c -> p a (s c)"),
                                   hf[:, :, 0:2, :].rearrange("p a s c -> p a (s c)"),
                                   hf[:, :, 2:4, :].rearrange("p a s c -> p a (s c)"), ALU.add).then_inc(half_used, 1)
                pool.wait_ge(half_used, n * TILES + i + 1 + LOOK)
                pool.tensor_tensor(mixed[:, :, :], quarter[:, :, 0, :], quarter[:, :, 1, :], ALU.add).then_inc(mixed_done, 1)
                pool.wait_ge(mixed_done, n * TILES + i + 1)
                if t == 0:
                    pool.wait_ge(xb_done, n * 2 + b + 2)
                    pool.wait_ge(stored[b], n * 16 + 16)
                pool.tensor_tensor(y_out[b][:, t, :, :], mixed[:, :, :], x_res[b][:, t, :, :], ALU.add).then_inc(out_done, 1)

            def round_(n, more):
                for i in range(TILES):
                    if i % TPI == 0:
                        input_and_bias(i // TPI, n)
                    finish(i, n)
                    if more and i == 3:
                        inverse_deviation(n + 1)
                    if more and 8 <= i < 8 + NP:
                        input_tails(n + 1, i - 8)

            pool.memset(cw_pair[:, :, :], 0.0).then_inc(cleared, 1)
            pool.memset(minus_half[:, :], -0.5)
            pool.memset(ones[:, :], 1.0)
            for edge in (0, PW + PAIRS):
                pool.memset(v_head[:, :, edge:edge + PW], 0.0)
                last = pool.memset(v_tail[:, :, edge:edge + PW], 0.0)
            last.then_inc(ready, 1)
            pool.wait_ge(ready, 1)
            pool.memset(quarter[:, 0, 0, 0:1], 0.0).then_inc(half_used, LOOK)
            pool.memset(mixed[:, 0, 0:1], 0.0).then_inc(out_done, 1)
            pool.memset(bias_part[:, 0, 0:1], 0.0).then_inc(xb_done, 1)
            for b in range(2):
                pool.memset(y_out[b][:, 0, 0, 0:1], 0.0).then_inc(stored[b], 16)
            pool.wait_ge(small_loaded, 16 * 5)
            inverse_deviation(0)
            with pool.Fori(0, ROUNDS - 1) as n:
                round_(n, True)
            round_(ROUNDS - 1, False)


def kernel(x, L0_conv_coupler_w, L0_conv_coupler_b, L0_conv_weight, L0_conv_bias):
    import numpy as np
    import concourse.bacc as bacc
    from concourse.bass_utils import run_bass_kernel_spmd

    x = np.asarray(x)
    x_pix = x.transpose(0, 2, 3, 1).reshape(IMAGES, TPI, P, 2 * C)
    weight = np.asarray(L0_conv_weight).transpose(1, 3, 4, 2, 0).reshape(C, K * K * N)
    same_group = np.kron(np.eye(P // 2, dtype=np.float32), np.ones((2, 2), np.float32))
    eye = np.eye(P, dtype=np.float32)
    matrices = np.stack([0.5 * same_group, eye - 0.5 * same_group, eye], axis=1)

    host = {
        "x": x,
        "x_pix": x_pix,
        "weight": weight,
        "bias": np.asarray(L0_conv_bias),
        "coupler_w": np.asarray(L0_conv_coupler_w).reshape(SETS, C).T,
        "coupler_b": np.asarray(L0_conv_coupler_b),
        "matrices": matrices,
    }
    host = {name: np.ascontiguousarray(a) for name, a in host.items()}
    nc = bacc.Bacc("TRN2", target_bir_lowering=False, num_devices=1)
    args = {name: nc.dram_tensor(name, a.shape, F32, kind="ExternalInput").ap() for name, a in host.items()}
    out = nc.dram_tensor("out", x_pix.shape, F32, kind="ExternalOutput").ap()
    program(nc, out=out, **args)
    got = run_bass_kernel_spmd(nc, [host], core_ids=[0]).results[0]["out"]
    return got.reshape(IMAGES, H, W, C).transpose(0, 3, 1, 2)
```

```python
from contextlib import ExitStack

from concourse import mybir

F32 = mybir.dt.float32
F16 = mybir.dt.float16
I32 = mybir.dt.int32
ALU = mybir.AluOpType
ACT = mybir.ActivationFunctionType
AX = mybir.AxisListType

P = 128
IMAGES, C, H, W = 8, 64, 48, 48
SETS, K = 8, 3
HW = H * W
ROUNDS = IMAGES // 2
PW = W // 2
PAIRS = H * PW
TPI = PAIRS // P
TILES = 2 * TPI
PADDED = (H + 2) * PW
N = SETS * C
POINTS = (1, 2, 0, 3)
NP = len(POINTS)
CHUNK = 384
CHUNKS = HW // CHUNK
LOADS = 2
FLAT = C * K * K * N // P // LOADS
EPS = 1e-5
X_SCALE = 512.0
W_TOP = 2.0 ** 14
TINY = 2.0 ** -100
PIX = 2 * TILES
LOOK = 2
SETS_OF_BANKS = 3

WARM = 8
W_STEPS = 11
PREP_CHAIN = 16
F_PARTS = 3


def program(nc, x, x_pix, weight, bias, coupler_w, coupler_b, matrices, out):
    with ExitStack() as ctx:
        def sb(name, shape, dt=F32):
            return ctx.enter_context(nc.sbuf_tensor(name, shape, dt))

        def sem(name):
            return ctx.enter_context(nc.semaphore(name))

        w_raw = sb("w_raw", [P, K, K, N])
        w_sum = sb("w_sum", [P, K, N])
        w_pts = sb("w_pts", [P, 2, K, N])
        w_head = sb("w_head", [P, NP, K, N], F16)
        w_tail01 = sb("w_tail01", [P, NP, N], F16)
        w_tail2 = sb("w_tail2", [P, NP, N], F16)
        w_max_part = sb("w_max_part", [P, LOADS])
        w_max = sb("w_max", [P, 2])
        w_pow2 = sb("w_pow2", [P, 2])
        w_top = sb("w_top", [1, 2])
        magnitude = sb("magnitude", [P, 2])
        inverse = sb("inverse", [P, 2])
        scale = sb("scale", [P, 2])
        half_scale = sb("half_scale", [P, 2])
        minus_half_scale = sb("minus_half_scale", [P, 2])
        undo = sb("undo", [P, 2])
        ones = sb("ones", [1, P])
        ones_exp = sb("ones_exp", [1, 1])
        cw_pair = sb("cw_pair", [P, 2, SETS])
        cw_pts = sb("cw_pts", [P, 2, 2, 2, 2 * SETS], F16)
        cb_all = sb("cb_all", [P, SETS])
        bias_all = sb("bias_all", [P, C])
        mats = sb("mats", [P, 3, P])
        mean_mat, diff_mat, ident = (mats[:, k, :] for k in range(3))
        minus_half = sb("minus_half", [P, 1])

        x_raw = sb("x_raw", [P, HW])
        x_norm = sb("x_norm", [P, HW])
        stats = sb("stats", [P, CHUNKS, 6])
        mean_var = sb("mean_var", [P, 2])
        group = sb("group", [P, 3])
        diff_sq = sb("diff_sq", [P, 1])
        var_eps = sb("var_eps", [P, 1])
        rstd = sb("rstd", [P, 1])
        norm_scale = sb("norm_scale", [P, 1])
        v_pts = sb("v_pts", [P, NP, PAIRS])
        v_head = sb("v_head", [P, NP, PADDED], F16)
        v_tail = sb("v_tail", [P, NP, PADDED], F16)
        logit = sb("logit", [P, PIX, SETS])
        top = sb("top", [P, PIX])
        total = sb("total", [P, PIX])
        mix = sb("mix", [P, PIX, SETS])
        sel_next = sb("sel_next", [P, PIX * (SETS + 1)])
        sel_now = sb("sel_now", [P, PIX * (SETS + 1)])

        op = [sb(f"op{b}", [P, 2, NP, PADDED], F16) for b in range(2)]

        m1_sb = sb("m1_sb", [P, LOOK, N])
        prod = sb("prod", [P, 2, SETS, C])
        half = sb("half", [P, LOOK, 2, SETS // 2, C])
        quarter = sb("quarter", [P, 2, SETS // 4, C])
        mixed = sb("mixed", [P, 2, C])
        x_res = [sb(f"x_res{b}", [P, TPI, 2, C]) for b in range(2)]
        bias_part = sb("bias_part", [P, TPI * 2, C])
        y_out = [sb(f"y_out{b}", [P, TPI, 2, C]) for b in range(2)]

        bank = [ctx.enter_context(nc.psum_tensor(f"bank{b}", [P, N], F32)) for b in range(2 * SETS_OF_BANKS)]
        side = ctx.enter_context(nc.psum_tensor("side", [P, N], F32))
        w_bank = ctx.enter_context(nc.psum_tensor("w_bank", [P, N], F32))
        logit_ps = side[:, 0:PIX * SETS]
        group_ps = side[:, PIX * SETS:PIX * SETS + 3]

        mats_loaded = sem("mats_loaded")
        small_loaded = sem("small_loaded")
        flat_loaded = [sem(f"flat_loaded{k}") for k in range(LOADS)]
        w_loaded = [sem(f"w_loaded{r}") for r in range(K)]
        ready = sem("ready")
        cleared = sem("cleared")
        w_bounds = sem("w_bounds")
        w_chain = sem("w_chain")
        w_col = sem("w_col")
        w_cast = sem("w_cast")
        w_sums = sem("w_sums")
        w_points = sem("w_points")
        w_heads = sem("w_heads")
        w_tails = sem("w_tails")

        c_heads = sem("c_heads")
        c_tails = sem("c_tails")

        x_loaded = [sem(f"x_loaded{k}") for k in range(LOADS)]
        prep = sem("prep")
        group_done = sem("group_done")
        rstd_done = sem("rstd_done")
        norm_done = sem("norm_done")
        v_done = sem("v_done")
        late_points = sem("late_points")
        edge_done = sem("edge_done")
        h_done = sem("h_done")
        t_done = sem("t_done")
        logit_done = sem("logit_done")
        exp_done = sem("exp_done")
        sel_done = sem("sel_done")
        sel_copied = sem("sel_copied")
        ops_in = [[sem(f"ops_in{b}_{g}") for g in range(2)] for b in range(2)]

        m1_done = sem("m1_done")
        m2_done = sem("m2_done")
        m1_copied = sem("m1_copied")
        seeded = sem("seeded")
        y_done = sem("y_done")
        prod_done = sem("prod_done")
        half_done = sem("half_done")
        half_used = sem("half_used")
        mixed_done = sem("mixed_done")
        out_done = sem("out_done")
        xres_in = [sem(f"xres_in{b}") for b in range(2)]
        bias_done = sem("bias_done")
        xb_done = sem("xb_done")
        stored = [sem(f"stored{b}") for b in range(2)]

        x_pair = x.rearrange("(n b) c h w -> n (b c) (h w)", b=2)
        x_pix_v = x_pix.rearrange("(n b) t p k -> n b p t k", b=2)
        out_v = out.rearrange("(n b) t p k -> n b p t k", b=2)

        sel_w = sel_now[:, 0:PIX * SETS].rearrange("p (q s) -> p q s", s=SETS)
        sel_sum = sel_now[:, PIX * SETS:PIX * (SETS + 1)]
        sel_next_w = sel_next[:, 0:PIX * SETS].rearrange("p (q s) -> p q s", s=SETS)
        sel_next_sum = sel_next[:, PIX * SETS:PIX * (SETS + 1)]

        def spread(ap, n):
            return ap.unsqueeze(2).to_broadcast([P, ap.shape[1], n])

        def v_count(m, k):
            return k if isinstance(m, int) and m == 0 else m * NP - 2 + k

        def point_operands(k):
            even, odd = (x_norm[:, :].rearrange("p (q a) -> p q a", a=2)[:, :, a] for a in range(2))
            e_rows, o_rows, v_rows = (v.rearrange("p (h w) -> p h w", w=PW) for v in (even, odd, v_pts[:, k, :]))
            return ((v_pts[:, 0, :], even, odd),
                    (v_pts[:, 1, :], odd, even),
                    (v_rows[:, :, 1:PW], o_rows[:, :, 0:PW - 1], o_rows[:, :, 1:PW]),
                    (v_rows[:, :, 0:PW - 1], e_rows[:, :, 1:PW], e_rows[:, :, 0:PW - 1]))[k]

        def w_flat(k):
            return w_pts[:, :, :, :].rearrange("p j r n -> p (j r n)")[:, k * FLAT:(k + 1) * FLAT]

        def x_part(m, k):
            cols = slice(k * (HW // LOADS), (k + 1) * (HW // LOADS))
            return x_raw[:, cols], x_pair[m, :, cols]

        block = ctx.enter_context(nc.Block())

        @block.sync
        def _(sp):
            def wait(signal, value):
                sp.wait_ge(signal, value)
                sp.nop(nofuse=True)

            def fill_ops(b, g, m):
                lo, pts = C * b, slice(2 * g, 2 * g + 2)
                heads = v_head[lo:lo + C, pts, :]
                wait(h_done, m * NP + 2 * g + 2)
                sp.dma_start(op[b][0:C, :, pts, :], heads.unsqueeze(1).to_broadcast([C, 2, 2, PADDED])) \
                    .then_inc(ops_in[b][g], 16)
                sp.dma_start(op[b][C:P, 1, pts, 0:PAIRS], heads[:, :, PW:PW + PAIRS]).then_inc(ops_in[b][g], 16)
                wait(t_done, m * NP + 2 * g + 2)
                sp.dma_start(op[b][C:P, 0, pts, :], v_tail[lo:lo + C, pts, :]).then_inc(ops_in[b][g], 16)

            def load_res(b, n):
                sp.dma_start(x_res[b].rearrange("p t a c -> p t (a c)"), x_pix_v[n, b, :, :, :]).then_inc(xres_in[b], 16)

            def store(b, n, t0, t1):
                wait(out_done, n * TILES + b * TPI + t1 + 1)
                sp.dma_start(out_v[n, b, :, t0:t1, :],
                             y_out[b][:, t0:t1, :, :].rearrange("p t a c -> p t (a c)")).then_inc(stored[b], 16)

            sp.dma_start(mats[:, :, :], matrices).then_inc(mats_loaded, 16)
            for k in range(LOADS):
                sp.dma_start(*x_part(0, k)).then_inc(x_loaded[k], 16)
            flat_src = weight.rearrange("c r n -> c (r n)").rearrange("c (h n) -> (c h) n", h=2)
            for k in range(LOADS):
                sp.dma_start(w_flat(k), flat_src[:, k * FLAT:(k + 1) * FLAT]).then_inc(flat_loaded[k], 16)
            for r in range(K):
                for half_p in range(2):
                    sp.dma_start(w_raw[C * half_p:C * half_p + C, r, :, :].rearrange("p b n -> p (b n)"),
                                 weight[:, r, :]).then_inc(w_loaded[r], 16)
            fill_ops(0, 0, 0)
            fill_ops(0, 1, 0)
            load_res(0, 0)

            def round_(n, more):
                wait(prod_done, n * 2 * TILES + 2 * SETS_OF_BANKS)
                fill_ops(1, 0, n)
                fill_ops(1, 1, n)
                wait(out_done, n * TILES + 1)
                load_res(1, n)
                store(0, n, 0, TPI)
                if more:
                    load_res(0, n + 1)
                    wait(prod_done, n * 2 * TILES + 2 * TPI + 2 * SETS_OF_BANKS)
                    fill_ops(0, 0, n + 1)
                    fill_ops(0, 1, n + 1)
                    store(1, n, 0, TPI)
                else:
                    store(1, n, 0, TPI - 2)
                    store(1, n, TPI - 2, TPI - 1)
                    store(1, n, TPI - 1, TPI)

            with sp.Fori(0, ROUNDS - 1) as n:
                round_(n, True)
            round_(ROUNDS - 1, False)
            wait(stored[0], 16 * (ROUNDS + 1))
            wait(stored[1], 16 * (ROUNDS + 3))

        @block.tensor
        def _(pe):
            def group_sums(m):
                if not isinstance(m, int) or m:
                    pe.wait_ge(prep, m * PREP_CHAIN)
                pe.wait_ge(prep, m * PREP_CHAIN + 2)
                nc.tensor.matmul(group_ps[:, 0:2], mean_mat[:, :], mean_var[:, :], start=True, stop=True)
                nc.tensor.matmul(group_ps[:, 2:3], diff_mat[:, :], mean_var[:, 0:1], start=True, stop=True) \
                    .then_inc(group_done, 1)

            def logits(m):
                pe.wait_ge(t_done, m * NP + 2)
                lg = logit_ps.rearrange("p (b t a s) -> p t a b s", b=2, t=TPI, a=2)
                for t in range(TPI):
                    at = slice(PW + t * P, PW + (t + 1) * P)
                    parts = [(v, k, c) for k in range(2) for v, c in ((v_head, 0), (v_head, 1), (v_tail, 0))]
                    for n, (v, k, c) in enumerate(parts):
                        last = nc.tensor.matmul(lg[:, t, :, :, :], v[:, k, at], cw_pts[:, k, c, :, :],
                                                start=n == 0, stop=n == len(parts) - 1)
                last.then_inc(logit_done, 1)

            def point(b, j, t, dst, fresh):
                at = t * P
                for r in range(K):
                    nc.tensor.matmul(dst, op[b][:, 0, j, at + r * PW:at + r * PW + P], w_head[:, j, r, :],
                                     start=fresh and r == 0, stop=False, skip_group_check=True)
                nc.tensor.matmul(dst, op[b][:, 0, j, at + 2 * PW:at + 2 * PW + P], w_tail2[:, j, :],
                                 start=False, stop=False, skip_group_check=True)
                return nc.tensor.matmul(dst, op[b][:, 1, j, at:at + P], w_tail01[:, j, :],
                                        start=False, stop=True, skip_group_check=True)

            def first_points(i, n, first=False):
                b, t, s = i // TPI, i % TPI, i % SETS_OF_BANKS
                if t == 0:
                    pe.wait_ge(ops_in[b][0], (n + 1) * 16 * F_PARTS)
                for a in range(2):
                    if first:
                        pe.wait_ge(w_tails, a + 1)
                    pe.wait_ge(prod_done, n * 2 * TILES + 2 * i + a + 1)
                    point(b, a, t, bank[2 * s + a][:, :], True).then_inc((m1_done, m2_done)[a], 1)

            def last_points(i, n):
                b, t, s = i // TPI, i % TPI, i % SETS_OF_BANKS
                if t == 0:
                    pe.wait_ge(ops_in[b][1], (n + 1) * 16 * F_PARTS)
                for a in range(2):
                    if i == 0:
                        pe.wait_ge(w_tails, 3 + a)
                    pe.wait_ge(seeded, n * 2 * TILES + 2 * i + a + 1 + 2 * LOOK)
                    point(b, 2 + a, t, bank[2 * s + a][:, :], False).then_inc(y_done, 1)

            def round_(n, more):
                for i in range(TILES):
                    if i + 1 < TILES:
                        first_points(i + 1, n)
                    elif more:
                        first_points(0, n + 1)
                    last_points(i, n)
                    if more and i == 4:
                        group_sums(n + 1)
                    if more and i == 13:
                        logits(n + 1)

            pe.wait_ge(mats_loaded, 16)
            group_sums(0)
            pe.wait_ge(ready, 1)
            pe.wait_ge(w_chain, 4)
            for k in range(2):
                last = nc.tensor.matmul(w_bank[0:1, k * P:(k + 1) * P], w_pow2[:, k:k + 1], ident[:, :], start=True, stop=True)
            last.then_inc(w_col, 1)
            pe.wait_ge(w_chain, 5)
            nc.tensor.matmul(w_bank[:, 2 * P:2 * P + 2], ones[0:1, :], w_top[0:1, :], start=True, stop=True).then_inc(w_cast, 1)
            pe.wait_ge(c_tails, 1)
            logits(0)
            for k in range(WARM):
                nc.tensor.matmul(w_bank[:, :], v_head[:, 0, 0:P], v_head[:, 0, 0:N], start=True, stop=True)
            first_points(0, 0, True)
            with pe.Fori(0, ROUNDS - 1) as n:
                round_(n, True)
            round_(ROUNDS - 1, False)

        @block.scalar
        def _(act):
            def input_heads(m, k, first=False):
                if first and k >= 2:
                    act.wait_ge(late_points, k - 1)
                else:
                    act.wait_ge(v_done, v_count(m, k + 1))
                if k >= 2:
                    v_rows = v_pts[:, k, :].rearrange("p (h w) -> p h w", w=PW)
                    x_rows = x_norm[:, :].rearrange("p (h w a) -> p h w a", w=PW, a=2)
                    col, a = ((0, 1), (PW - 1, 0))[k - 2]
                    act.activation(v_rows[:, :, col:col + 1], x_rows[:, :, col:col + 1, a], ACT.Copy, scale=-1.0) \
                        .then_inc(edge_done, 1)
                    act.wait_ge(edge_done, m * 2 + k - 1)
                if not first:
                    for b in range(2):
                        act.wait_ge(ops_in[b][k // 2], m * 16 * F_PARTS)
                    act.wait_ge(logit_done, m)
                act.activation(v_head[:, k, PW:PW + PAIRS], v_pts[:, k, :], ACT.Copy).then_inc(h_done, 1)

            def exponentials(m):
                act.wait_ge(prep, m * PREP_CHAIN + 9)
                act.activation(mix[:, :, :], logit[:, :, :], ACT.Exp).then_inc(exp_done, 1)

            def round_(n, more):
                for i in range(TILES):
                    act.wait_ge(m1_done, n * TILES + i + 1)
                    act.wait_ge(seeded, n * 2 * TILES + 2 * i + 2)
                    act.activation(m1_sb[:, i % LOOK, :], bank[2 * (i % SETS_OF_BANKS)][:, :], ACT.Copy) \
                        .then_inc(m1_copied, 1)
                    if more and i == 2:
                        act.wait_ge(norm_done, n + 1)
                        for k in range(LOADS):
                            act.dma_start(*x_part(n + 1, k)).then_inc(x_loaded[k], 16)
                    if more and 10 <= i < 10 + NP:
                        input_heads(n + 1, i - 10)
                    if more and i == 15:
                        exponentials(n + 1)

            def w_heads_of(k):
                if k < 2:
                    act.wait_ge(w_points, k + 1)
                src = w_pts[:, k, :, :] if k < 2 else w_raw[:, :, 2 * (k - 2), :]
                act.activation(w_head[:, k, :, :], src, ACT.Copy,
                               scale=half_scale[:, 0:1] if k < 2 else scale[:, 0:1]).then_inc(w_heads, 1)

            act.dma_start(bias_all[:, :], bias.partition_broadcast(P)).then_inc(small_loaded, 16)
            act.dma_start(cb_all[:, :], coupler_b.partition_broadcast(P)).then_inc(small_loaded, 16)
            act.wait_ge(cleared, 1)
            for b in range(2):
                act.dma_start(cw_pair[C * b:C * b + C, b, :], coupler_w).then_inc(small_loaded, 16)
            act.wait_ge(ready, 1)
            act.activation(ones_exp[:, :], ones[0:1, 0:1], ACT.Exp)
            for k in range(LOADS):
                act.wait_ge(flat_loaded[k], 16)
                act.activation(w_flat(k), w_flat(k), ACT.Abs, accum_out=w_max_part[:, k:k + 1]).then_inc(w_bounds, 1)
            for k in range(2):
                input_heads(0, k, True)
            act.wait_ge(w_chain, W_STEPS)
            cw = cw_pair[:, :, :].rearrange("p b s -> p (b s)")
            for k, a, by in ((0, 0, half_scale), (0, 1, half_scale), (1, 0, minus_half_scale), (1, 1, half_scale)):
                last = act.activation(cw_pts[:, k, 0, a, :], cw, ACT.Copy, scale=by[:, 1:2])
            last.then_inc(c_heads, 1)
            input_heads(0, 2, True)
            w_heads_of(0)
            input_heads(0, 3, True)
            w_heads_of(1)
            w_heads_of(2)
            w_heads_of(3)
            exponentials(0)
            with act.Fori(0, ROUNDS - 1) as n:
                round_(n, True)
            round_(ROUNDS - 1, False)

        @block.vector
        def _(dve):
            def statistics(m):
                for k in range(CHUNKS):
                    if k % (CHUNKS // LOADS) == 0:
                        dve.wait_ge(x_loaded[k // (CHUNKS // LOADS)], (m + 1) * 16)
                    last = dve.bn_stats(stats[:, k, :], x_raw[:, k * CHUNK:(k + 1) * CHUNK])
                last.then_inc(prep, 1)

            def aggregate(m):
                dve.wait_ge(prep, m * PREP_CHAIN + 1)
                dve.nop(nofuse=True)
                dve.bn_aggr(mean_var[:, :], stats[:, :, :]).then_inc(prep, 1)

            def group_variance(m):
                dve.wait_ge(group_done, m + 1)
                dve.tensor_copy(group[:, :], group_ps).then_inc(prep, 1)
                dve.wait_ge(prep, m * PREP_CHAIN + 3)
                dve.tensor_tensor(diff_sq[:, :], group[:, 2:3], group[:, 2:3], ALU.mult).then_inc(prep, 1)
                dve.wait_ge(prep, m * PREP_CHAIN + 4)
                dve.scalar_tensor_tensor(var_eps[:, :], group[:, 1:2], EPS, diff_sq[:, :], ALU.add, ALU.add).then_inc(prep, 1)

            def normalise(m, first=False):
                dve.wait_ge(rstd_done, m + 1)
                dve.tensor_scalar(norm_scale[:, :], rstd[:, :], X_SCALE, None, ALU.mult).then_inc(prep, 1)
                dve.wait_ge(prep, m * PREP_CHAIN + 6)
                if not first:
                    dve.wait_ge(v_done, v_count(m, 0))
                    dve.wait_ge(edge_done, m * 2)
                dve.tensor_scalar(x_norm[:, :], x_raw[:, :], group[:, 0:1], norm_scale[:, 0:1],
                                  ALU.subtract, ALU.mult).then_inc(norm_done, 1)

            def input_point(m, k, first=False):
                dve.wait_ge(norm_done, m + 1)
                if not first:
                    dve.wait_ge(t_done, m * NP - NP + k + 1)
                v_out, left, right = point_operands(k)
                dve.tensor_tensor(v_out, left, right, ALU.add if k == 0 else ALU.subtract).then_inc(v_done, 1)

            def softmax_in(m):
                dve.wait_ge(logit_done, m + 1)
                dve.scalar_tensor_tensor(logit[:, :, :], logit_ps.rearrange("p (q s) -> p q s", s=SETS), undo[:, 1:2],
                                         cb_all[:, :].unsqueeze(1).to_broadcast([P, PIX, SETS]), ALU.mult, ALU.add) \
                    .then_inc(prep, 1)
                dve.wait_ge(prep, m * PREP_CHAIN + 7)
                dve.tensor_reduce(top[:, :], logit[:, :, :], axis=AX.X, op=ALU.max).then_inc(prep, 1)
                dve.wait_ge(prep, m * PREP_CHAIN + 8)
                dve.tensor_tensor(logit[:, :, :], logit[:, :, :], spread(top[:, :], SETS), ALU.subtract).then_inc(prep, 1)

            def softmax_out(m):
                dve.wait_ge(exp_done, m + 1)
                dve.tensor_reduce(total[:, :], mix[:, :, :], axis=AX.X, op=ALU.add).then_inc(prep, 1)
                dve.wait_ge(prep, m * PREP_CHAIN + 10)
                dve.reciprocal(total[:, :], total[:, :]).then_inc(prep, 1)
                dve.wait_ge(prep, m * PREP_CHAIN + 11)
                dve.tensor_tensor(logit[:, :, :], mix[:, :, :], spread(total[:, :], SETS), ALU.mult).then_inc(prep, 1)

            def renormalise(m):
                dve.wait_ge(prep, m * PREP_CHAIN + 12)
                dve.tensor_reduce(top[:, :], logit[:, :, :], axis=AX.X, op=ALU.add).then_inc(prep, 1)
                dve.wait_ge(prep, m * PREP_CHAIN + 13)
                dve.reciprocal(top[:, :], top[:, :]).then_inc(prep, 1)
                dve.wait_ge(prep, m * PREP_CHAIN + 14)
                dve.tensor_tensor(mix[:, :, :], logit[:, :, :], spread(top[:, :], SETS), ALU.mult).then_inc(prep, 1)
                dve.wait_ge(prep, m * PREP_CHAIN + 15)
                dve.tensor_reduce(sel_next_sum, mix[:, :, :], axis=AX.X, op=ALU.add).then_inc(prep, 1)
                dve.tensor_scalar(sel_next_w, mix[:, :, :], undo[:, 0:1], None, ALU.mult).then_inc(sel_done, 1)

            def seed(i, n):
                plus, minus = (bank[2 * (i % SETS_OF_BANKS) + a] for a in range(2))
                m1 = m1_sb[:, i % LOOK, :]
                dve.wait_ge(m2_done, n * TILES + i + 1)
                dve.wait_ge(m1_copied, n * TILES + i + 1)
                dve.tensor_tensor(plus[:, :], minus[:, :], m1, ALU.add).then_inc(seeded, 1)
                dve.tensor_tensor(minus[:, :], m1, minus[:, :], ALU.subtract).then_inc(seeded, 1)

            def multiply(i, n):
                for a in range(2):
                    dve.wait_ge(half_done, n * 2 * TILES + 2 * i + a + 1)
                    dve.wait_ge(y_done, n * 2 * TILES + 2 * i + a + 1)
                    dve.tensor_tensor(prod[:, a, :, :],
                                      bank[2 * (i % SETS_OF_BANKS) + a][:, :].rearrange("p (s c) -> p s c", c=C),
                                      spread(sel_w[:, 2 * i + a, :], C), ALU.mult).then_inc(prod_done, 1)

            def halve(i, n):
                dve.wait_ge(half_used, n * TILES + i + 1)
                for a in range(2):
                    dve.wait_ge(prod_done, n * 2 * TILES + 2 * i + a + 1 + 2 * SETS_OF_BANKS)
                    dve.tensor_tensor(half[:, i % LOOK, a, :, :], prod[:, a, 0:SETS // 2, :],
                                      prod[:, a, SETS // 2:SETS, :], ALU.add).then_inc(half_done, 1)

            def take_selection(n):
                dve.wait_ge(sel_done, n + 1)
                if not isinstance(n, int) or n:
                    dve.wait_ge(prod_done, n * 2 * TILES + 2 * SETS_OF_BANKS)
                    dve.wait_ge(xb_done, n * 2)
                dve.tensor_copy(sel_now[:, :], sel_next[:, :]).then_inc(sel_copied, 1)

            def round_(n, more):
                for i in range(TILES):
                    if i + 1 < TILES:
                        seed(i + 1, n)
                    elif more:
                        seed(0, n + 1)
                    if i == 0:
                        dve.wait_ge(sel_copied, n + 1)
                    multiply(i, n)
                    halve(i, n)
                    if more and i == 2:
                        statistics(n + 1)
                        aggregate(n + 1)
                    if more and i == 5:
                        group_variance(n + 1)
                    if more and i == 7:
                        normalise(n + 1)
                    if more and 8 <= i < 8 + NP:
                        input_point(n + 1, i - 8)
                    if more and i == 14:
                        softmax_in(n + 1)
                    if more and i == 15:
                        softmax_out(n + 1)
                    if more and i == 16:
                        renormalise(n + 1)
                if more:
                    take_selection(n + 1)

            dve.memset(diff_sq[:, :], 0.0).then_inc(seeded, 2 * LOOK)
            dve.memset(var_eps[:, :], 0.0).then_inc(prod_done, 2 * SETS_OF_BANKS)
            dve.memset(norm_scale[:, :], 0.0).then_inc(half_done, 2)
            def w_point(k):
                dve.tensor_tensor(w_pts[:, k, :, :], w_sum[:, :, :], w_raw[:, :, 1, :],
                                  (ALU.add, ALU.subtract)[k]).then_inc(w_points, 1)

            def w_tails_of(k):
                dve.wait_ge(w_heads, k + 1)
                src = w_pts[:, k, :, :] if k < 2 else w_raw[:, :, 2 * (k - 2), :]
                for lo, hi, r, tail in ((0, C, 0, w_tail01), (C, P, 1, w_tail01), (0, P, 2, w_tail2)):
                    by = half_scale[lo:hi, 0:1] if k < 2 else scale[lo:hi, 0:1]
                    last = dve.scalar_tensor_tensor(tail[lo:hi, k, :], src[lo:hi, r, :], by, w_head[lo:hi, k, r, :],
                                                    ALU.mult, ALU.subtract)
                last.then_inc(w_tails, 1)

            def c_tails_of():
                dve.wait_ge(c_heads, 1)
                cw = cw_pair[:, :, :].rearrange("p b s -> p (b s)")
                for k, a, by in ((0, 0, half_scale), (0, 1, half_scale), (1, 0, minus_half_scale), (1, 1, half_scale)):
                    last = dve.scalar_tensor_tensor(cw_pts[:, k, 1, a, :], cw, by[:, 1:2], cw_pts[:, k, 0, a, :],
                                                    ALU.mult, ALU.subtract)
                last.then_inc(c_tails, 1)

            statistics(0)
            aggregate(0)
            group_variance(0)
            dve.wait_ge(small_loaded, 16 * 4)
            dve.tensor_reduce(w_max[:, 1:2], cw_pair[:, :, :].rearrange("p b s -> p (b s)"), axis=AX.X, op=ALU.max,
                              apply_absolute_value=True).then_inc(w_chain, 1)
            dve.wait_ge(w_bounds, LOADS)
            dve.tensor_reduce(w_max[:, 0:1], w_max_part[:, :], axis=AX.X, op=ALU.max).then_inc(w_chain, 1)
            dve.wait_ge(w_chain, 2)
            dve.tensor_scalar(w_max[:, :], w_max[:, :], TINY, None, ALU.max).then_inc(w_chain, 1)
            dve.wait_ge(w_chain, 3)
            dve.tensor_scalar(w_pow2[:, :].bitcast(I32), w_max[:, :].bitcast(I32), 0x7F800000, None,
                              ALU.bitwise_and).then_inc(w_chain, 1)
            normalise(0, True)
            input_point(0, 0, True)
            dve.wait_ge(w_col, 1)
            dve.tensor_reduce(w_top[0:1, :], w_bank[0:1, 0:2 * P].rearrange("p (k q) -> p k q", k=2), axis=AX.X,
                              op=ALU.max).then_inc(w_chain, 1)
            input_point(0, 1, True)
            dve.wait_ge(w_cast, 1)
            dve.tensor_copy(magnitude[:, :], w_bank[:, 2 * P:2 * P + 2]).then_inc(w_chain, 1)
            dve.wait_ge(w_chain, 6)
            dve.reciprocal(inverse[:, :], magnitude[:, :]).then_inc(w_chain, 1)
            dve.tensor_scalar(undo[:, :], magnitude[:, :], 1.0 / (W_TOP * X_SCALE), None, ALU.mult).then_inc(w_chain, 1)
            dve.wait_ge(w_chain, 7)
            for dst, by in ((half_scale, W_TOP / 2), (minus_half_scale, -W_TOP / 2), (scale, W_TOP)):
                dve.tensor_scalar(dst[:, :], inverse[:, :], by, None, ALU.mult).then_inc(w_chain, 1)
            dve.wait_ge(ready, 1)
            for k in range(2):
                dve.wait_ge(h_done, k + 1)
                dve.tensor_tensor(v_tail[:, k, PW:PW + PAIRS], v_pts[:, k, :], v_head[:, k, PW:PW + PAIRS],
                                  ALU.subtract).then_inc(t_done, 1)
            c_tails_of()
            dve.wait_ge(w_sums, K)
            w_point(0)
            w_point(1)
            dve.wait_ge(w_chain, W_STEPS)
            w_tails_of(0)
            w_tails_of(1)
            softmax_in(0)
            w_tails_of(2)
            seed(0, 0)
            w_tails_of(3)
            softmax_out(0)
            renormalise(0)
            take_selection(0)
            with dve.Fori(0, ROUNDS - 1) as n:
                round_(n, True)
            round_(ROUNDS - 1, False)

        @block.gpsimd
        def _(pool):
            def inverse_deviation(m):
                pool.wait_ge(prep, m * PREP_CHAIN + 5)
                pool.tensor_tensor(rstd[:, :], var_eps[:, :], minus_half[:, :], ALU.pow).then_inc(rstd_done, 1)

            def input_tails(m, k, first=False):
                pool.wait_ge(h_done, m * NP + k + 1)
                if first:
                    pool.wait_ge(t_done, k)
                for b in range(0 if first else 2):
                    pool.wait_ge(ops_in[b][k // 2], m * 16 * F_PARTS)
                if not first:
                    pool.wait_ge(logit_done, m)
                pool.tensor_tensor(v_tail[:, k, PW:PW + PAIRS], v_pts[:, k, :], v_head[:, k, PW:PW + PAIRS],
                                   ALU.subtract).then_inc(t_done, 1)

            def input_and_bias(b, n):
                pool.wait_ge(sel_copied, n + 1)
                q0 = b * TPI * 2
                pool.tensor_tensor(bias_part[:, :, :], bias_all[:, :].unsqueeze(1).to_broadcast([P, TPI * 2, C]),
                                   spread(sel_sum[:, q0:q0 + TPI * 2], C), ALU.mult).then_inc(bias_done, 1)
                pool.wait_ge(xres_in[b], (n + 1) * 16)
                pool.wait_ge(bias_done, n * 2 + b + 1)
                xr = x_res[b][:, :, :, :].rearrange("p t a c -> p (t a) c")
                pool.tensor_tensor(xr, xr, bias_part[:, :, :], ALU.add).then_inc(xb_done, 1)

            def finish(i, n):
                b, t = i // TPI, i % TPI
                pool.wait_ge(half_done, n * 2 * TILES + 2 * i + 2 + 2)
                hf = half[:, i % LOOK, :, :, :]
                pool.tensor_tensor(quarter[:, :, :, :].rearrange("p a s c -> p a (s c)"),
                                   hf[:, :, 0:2, :].rearrange("p a s c -> p a (s c)"),
                                   hf[:, :, 2:4, :].rearrange("p a s c -> p a (s c)"), ALU.add).then_inc(half_used, 1)
                pool.wait_ge(half_used, n * TILES + i + 1 + LOOK)
                pool.tensor_tensor(mixed[:, :, :], quarter[:, :, 0, :], quarter[:, :, 1, :], ALU.add).then_inc(mixed_done, 1)
                pool.wait_ge(mixed_done, n * TILES + i + 1)
                if t == 0:
                    pool.wait_ge(xb_done, n * 2 + b + 1)
                    pool.wait_ge(stored[b], n * 16 + 16)
                pool.tensor_tensor(y_out[b][:, t, :, :], mixed[:, :, :], x_res[b][:, t, :, :], ALU.add).then_inc(out_done, 1)

            def round_(n, more):
                for i in range(TILES):
                    if i % TPI == 0:
                        input_and_bias(i // TPI, n)
                    finish(i, n)
                    if more and i == 4:
                        inverse_deviation(n + 1)
                    if more and 9 <= i < 9 + NP:
                        input_tails(n + 1, i - 9)

            pool.memset(cw_pair[:, :, :], 0.0).then_inc(cleared, 1)
            pool.memset(minus_half[:, :], -0.5)
            pool.memset(ones[:, :], 1.0)
            for edge in (0, PW + PAIRS):
                pool.memset(v_head[:, :, edge:edge + PW], 0.0)
                last = pool.memset(v_tail[:, :, edge:edge + PW], 0.0)
            last.then_inc(ready, 1)
            pool.wait_ge(ready, 1)
            pool.memset(quarter[:, 0, 0, 0:1], 0.0).then_inc(half_used, LOOK)
            pool.memset(mixed[:, 0, 0:1], 0.0).then_inc(out_done, 1)
            for b in range(2):
                pool.memset(y_out[b][:, 0, 0, 0:1], 0.0).then_inc(stored[b], 16)
            def row_sum(r):
                pool.wait_ge(w_loaded[r], 16 * 2)
                pool.tensor_tensor(w_sum[:, r, :], w_raw[:, r, 0, :], w_raw[:, r, 2, :], ALU.add).then_inc(w_sums, 1)

            inverse_deviation(0)
            def late_point(k):
                pool.wait_ge(norm_done, 1)
                v_out, left, right = point_operands(k)
                pool.tensor_tensor(v_out, left, right, ALU.subtract).then_inc(late_points, 1)

            row_sum(0)
            late_point(2)
            row_sum(1)
            row_sum(2)
            late_point(3)
            for k in range(2, NP):
                input_tails(0, k, True)
            pool.wait_ge(small_loaded, 16 * 4)
            with pool.Fori(0, ROUNDS - 1) as n:
                round_(n, True)
            round_(ROUNDS - 1, False)


def kernel(x, L0_conv_coupler_w, L0_conv_coupler_b, L0_conv_weight, L0_conv_bias):
    import numpy as np
    import concourse.bacc as bacc
    from concourse.bass_utils import run_bass_kernel_spmd

    x = np.asarray(x)
    x_pix = x.transpose(0, 2, 3, 1).reshape(IMAGES, TPI, P, 2 * C)
    weight = np.asarray(L0_conv_weight).transpose(1, 3, 4, 2, 0).reshape(C, K, K * N)
    same_group = np.kron(np.eye(P // 2, dtype=np.float32), np.ones((2, 2), np.float32))
    eye = np.eye(P, dtype=np.float32)
    matrices = np.stack([0.5 * same_group, eye - 0.5 * same_group, eye], axis=1)

    host = {
        "x": x,
        "x_pix": x_pix,
        "weight": weight,
        "bias": np.asarray(L0_conv_bias),
        "coupler_w": np.asarray(L0_conv_coupler_w).reshape(SETS, C).T,
        "coupler_b": np.asarray(L0_conv_coupler_b),
        "matrices": matrices,
    }
    host = {name: np.ascontiguousarray(a) for name, a in host.items()}
    nc = bacc.Bacc("TRN2", target_bir_lowering=False, num_devices=1)
    args = {name: nc.dram_tensor(name, a.shape, F32, kind="ExternalInput").ap() for name, a in host.items()}
    out = nc.dram_tensor("out", x_pix.shape, F32, kind="ExternalOutput").ap()
    program(nc, out=out, **args)
    got = run_bass_kernel_spmd(nc, [host], core_ids=[0]).results[0]["out"]
    return got.reshape(IMAGES, H, W, C).transpose(0, 3, 1, 2)
```

```python
from contextlib import ExitStack

from concourse import mybir

F32 = mybir.dt.float32
F16 = mybir.dt.float16
I32 = mybir.dt.int32
ALU = mybir.AluOpType
ACT = mybir.ActivationFunctionType
AX = mybir.AxisListType

P = 128
IMAGES, C, H, W = 8, 64, 48, 48
SETS, K = 8, 3
HW = H * W
ROUNDS = IMAGES // 2
PW = W // 2
PAIRS = H * PW
TPI = PAIRS // P
TILES = 2 * TPI
PADDED = (H + 2) * PW
N = SETS * C
POINTS = (1, 2, 0, 3)
NP = len(POINTS)
CHUNK = 384
CHUNKS = HW // CHUNK
LOADS = 3
EPS = 1e-5
X_SCALE = 512.0
W_TOP = 2.0 ** 14
TINY = 2.0 ** -100
PIX = 2 * TILES
LOOK = 2
SETS_OF_BANKS = 3

WARM = 8
W_STEPS = 11
PREP_CHAIN = 16
F_PARTS = 3


def program(nc, x, x_pix, weight, bias, coupler_w, coupler_b, matrices, out):
    with ExitStack() as ctx:
        def sb(name, shape, dt=F32):
            return ctx.enter_context(nc.sbuf_tensor(name, shape, dt))

        def sem(name):
            return ctx.enter_context(nc.semaphore(name))

        w_raw = sb("w_raw", [P, K, K, N])
        w_sum = sb("w_sum", [P, K, N])
        w_pts = sb("w_pts", [P, 2, K, N])
        w_head = sb("w_head", [P, NP, K, N], F16)
        w_tail01 = sb("w_tail01", [P, NP, N], F16)
        w_tail2 = sb("w_tail2", [P, NP, N], F16)
        w_max_part = sb("w_max_part", [P, K])
        w_max = sb("w_max", [P, 2])
        w_pow2 = sb("w_pow2", [P, 2])
        w_top = sb("w_top", [1, 2])
        magnitude = sb("magnitude", [P, 2])
        inverse = sb("inverse", [P, 2])
        scale = sb("scale", [P, 2])
        half_scale = sb("half_scale", [P, 2])
        minus_half_scale = sb("minus_half_scale", [P, 2])
        undo = sb("undo", [P, 2])
        ones = sb("ones", [1, P])
        ones_exp = sb("ones_exp", [1, 1])
        cw_pair = sb("cw_pair", [P, 2, SETS])
        cw_pts = sb("cw_pts", [P, 2, 2, 2, 2 * SETS], F16)
        cb_all = sb("cb_all", [P, SETS])
        bias_all = sb("bias_all", [P, C])
        mats = sb("mats", [P, 3, P])
        mean_mat, diff_mat, ident = (mats[:, k, :] for k in range(3))
        minus_half = sb("minus_half", [P, 1])

        x_raw = sb("x_raw", [P, HW])
        x_norm = sb("x_norm", [P, HW])
        stats = sb("stats", [P, CHUNKS, 6])
        mean_var = sb("mean_var", [P, 2])
        group = sb("group", [P, 3])
        diff_sq = sb("diff_sq", [P, 1])
        var_eps = sb("var_eps", [P, 1])
        rstd = sb("rstd", [P, 1])
        norm_scale = sb("norm_scale", [P, 1])
        v_pts = sb("v_pts", [P, NP, PAIRS])
        v_head = sb("v_head", [P, NP, PADDED], F16)
        v_tail = sb("v_tail", [P, NP, PADDED], F16)
        logit = sb("logit", [P, PIX, SETS])
        top = sb("top", [P, PIX])
        total = sb("total", [P, PIX])
        mix = sb("mix", [P, PIX, SETS])
        sel_next = sb("sel_next", [P, PIX * (SETS + 1)])
        sel_now = sb("sel_now", [P, PIX * (SETS + 1)])

        op = [sb(f"op{b}", [P, 2, NP, PADDED], F16) for b in range(2)]

        m1_sb = sb("m1_sb", [P, LOOK, N])
        prod = sb("prod", [P, 2, SETS, C])
        half = sb("half", [P, LOOK, 2, SETS // 2, C])
        quarter = sb("quarter", [P, 2, SETS // 4, C])
        mixed = sb("mixed", [P, 2, C])
        x_res = [sb(f"x_res{b}", [P, TPI, 2, C]) for b in range(2)]
        last_quarter = sb("last_quarter", [P, 2, SETS // 4, C])
        last_mixed = sb("last_mixed", [P, 2, C])
        bias_part = sb("bias_part", [P, TPI * 2, C])
        y_out = [sb(f"y_out{b}", [P, TPI, 2, C]) for b in range(2)]

        bank = [ctx.enter_context(nc.psum_tensor(f"bank{b}", [P, N], F32)) for b in range(2 * SETS_OF_BANKS)]
        side = ctx.enter_context(nc.psum_tensor("side", [P, N], F32))
        w_bank = ctx.enter_context(nc.psum_tensor("w_bank", [P, N], F32))
        logit_ps = side[:, 0:PIX * SETS]
        group_ps = side[:, PIX * SETS:PIX * SETS + 3]

        mats_loaded = sem("mats_loaded")
        small_loaded = sem("small_loaded")
        w_loaded = [sem(f"w_loaded{r}") for r in range(K)]
        ready = sem("ready")
        cleared = sem("cleared")
        w_bounds = sem("w_bounds")
        w_chain = sem("w_chain")
        w_col = sem("w_col")
        w_cast = sem("w_cast")
        w_sums = sem("w_sums")
        w_point1 = sem("w_point1")
        w_point2 = sem("w_point2")
        w_heads = sem("w_heads")
        w_tails = sem("w_tails")

        c_heads = sem("c_heads")
        c_tails = sem("c_tails")

        x_loaded = [sem(f"x_loaded{k}") for k in range(LOADS)]
        prep = sem("prep")
        group_done = sem("group_done")
        rstd_done = sem("rstd_done")
        norm_done = sem("norm_done")
        v_done = sem("v_done")
        late_points = sem("late_points")
        edge_done = sem("edge_done")
        h_done = sem("h_done")
        t_done = sem("t_done")
        logit_done = sem("logit_done")
        exp_done = sem("exp_done")
        sel_done = sem("sel_done")
        sel_copied = sem("sel_copied")
        ops_in = [[sem(f"ops_in{b}_{g}") for g in range(2)] for b in range(2)]

        m1_done = sem("m1_done")
        m2_done = sem("m2_done")
        m1_copied = sem("m1_copied")
        seeded = sem("seeded")
        y_done = sem("y_done")
        prod_done = sem("prod_done")
        half_done = sem("half_done")
        half_used = sem("half_used")
        mixed_done = sem("mixed_done")
        out_done = sem("out_done")
        xres_in = [sem(f"xres_in{b}") for b in range(2)]
        bias_done = sem("bias_done")
        xb_done = sem("xb_done")
        last_steps = [sem(f"last_steps{a}") for a in range(2)]
        stored = [sem(f"stored{b}") for b in range(2)]

        x_pair = x.rearrange("(n b) c h w -> n (b c) (h w)", b=2)
        x_pix_v = x_pix.rearrange("(n b) t p k -> n b p t k", b=2)
        out_v = out.rearrange("(n b) t p k -> n b p t k", b=2)

        sel_now_parts, sel_next_parts = ((sel[:, 0:PIX * SETS].rearrange("p (q s) -> p q s", s=SETS),
                                          sel[:, PIX * SETS:PIX * (SETS + 1)]) for sel in (sel_now, sel_next))
        sel_w, sel_sum = sel_now_parts

        def spread(ap, n):
            return ap.unsqueeze(2).to_broadcast([P, ap.shape[1], n])

        def v_count(m, k):
            return k if isinstance(m, int) and m == 0 else m * NP - 2 + k

        def point_operands(k):
            even, odd = (x_norm[:, :].rearrange("p (q a) -> p q a", a=2)[:, :, a] for a in range(2))
            e_rows, o_rows, v_rows = (v.rearrange("p (h w) -> p h w", w=PW) for v in (even, odd, v_pts[:, k, :]))
            return ((v_pts[:, 0, :], even, odd),
                    (v_pts[:, 1, :], odd, even),
                    (v_rows[:, :, 1:PW], o_rows[:, :, 0:PW - 1], o_rows[:, :, 1:PW]),
                    (v_rows[:, :, 0:PW - 1], e_rows[:, :, 1:PW], e_rows[:, :, 0:PW - 1]))[k]

        def x_part(m, k):
            cols = slice(k * (HW // LOADS), (k + 1) * (HW // LOADS))
            return x_raw[:, cols], x_pair[m, :, cols]

        block = ctx.enter_context(nc.Block())

        @block.sync
        def _(sp):
            def wait(signal, value):
                sp.wait_ge(signal, value)
                sp.nop(nofuse=True)

            def fill_ops(b, g, m):
                lo, pts = C * b, slice(2 * g, 2 * g + 2)
                heads = v_head[lo:lo + C, pts, :]
                wait(h_done, m * NP + 2 * g + 2)
                sp.dma_start(op[b][0:C, :, pts, :], heads.unsqueeze(1).to_broadcast([C, 2, 2, PADDED])) \
                    .then_inc(ops_in[b][g], 16)
                sp.dma_start(op[b][C:P, 1, pts, 0:PAIRS], heads[:, :, PW:PW + PAIRS]).then_inc(ops_in[b][g], 16)
                wait(t_done, m * NP + 2 * g + 2)
                sp.dma_start(op[b][C:P, 0, pts, :], v_tail[lo:lo + C, pts, :]).then_inc(ops_in[b][g], 16)

            def load_res(b, n):
                sp.dma_start(x_res[b].rearrange("p t a c -> p t (a c)"), x_pix_v[n, b, :, :, :]).then_inc(xres_in[b], 16)

            def last_store():
                sp.dma_start(out_v[ROUNDS - 1, 1, :, TPI - 1, :],
                             y_out[1][:, TPI - 1, :, :].rearrange("p a c -> p (a c)")).then_inc(stored[1], 16)

            def store(b, n, t0, t1):
                wait(out_done, n * TILES + b * TPI + t1 + 1)
                sp.dma_start(out_v[n, b, :, t0:t1, :],
                             y_out[b][:, t0:t1, :, :].rearrange("p t a c -> p t (a c)")).then_inc(stored[b], 16)

            for k in range(LOADS):
                sp.dma_start(*x_part(0, k)).then_inc(x_loaded[k], 16)
            sp.dma_start(mats[:, :, :], matrices).then_inc(mats_loaded, 16)
            for r in range(K):
                for half_p in range(2):
                    sp.dma_start(w_raw[C * half_p:C * half_p + C, r, :, :].rearrange("p b n -> p (b n)"),
                                 weight[:, r, :]).then_inc(w_loaded[r], 16)
            fill_ops(0, 0, 0)
            fill_ops(0, 1, 0)
            load_res(0, 0)

            def round_(n, more):
                wait(prod_done, n * 2 * TILES + 2 * SETS_OF_BANKS)
                fill_ops(1, 0, n)
                fill_ops(1, 1, n)
                wait(out_done, n * TILES + 1)
                load_res(1, n)
                store(0, n, 0, TPI)
                if more:
                    load_res(0, n + 1)
                    wait(prod_done, n * 2 * TILES + 2 * TPI + 2 * SETS_OF_BANKS)
                    fill_ops(0, 0, n + 1)
                    fill_ops(0, 1, n + 1)
                    store(1, n, 0, TPI)
                else:
                    store(1, n, 0, TPI - 2)
                    store(1, n, TPI - 2, TPI - 1)
                    for a in range(2):
                        wait(last_steps[a], 3)
                    last_store()

            with sp.Fori(0, ROUNDS - 1) as n:
                round_(n, True)
            round_(ROUNDS - 1, False)
            wait(stored[0], 16 * (ROUNDS + 1))
            wait(stored[1], 16 * (ROUNDS + 3))

        @block.tensor
        def _(pe):
            def group_sums(m):
                if not isinstance(m, int) or m:
                    pe.wait_ge(prep, m * PREP_CHAIN)
                pe.wait_ge(prep, m * PREP_CHAIN + 2)
                nc.tensor.matmul(group_ps[:, 0:2], mean_mat[:, :], mean_var[:, :], start=True, stop=True)
                nc.tensor.matmul(group_ps[:, 2:3], diff_mat[:, :], mean_var[:, 0:1], start=True, stop=True) \
                    .then_inc(group_done, 1)

            def logits(m):
                pe.wait_ge(t_done, m * NP + 2)
                lg = logit_ps.rearrange("p (b t a s) -> p t a b s", b=2, t=TPI, a=2)
                for t in range(TPI):
                    at = slice(PW + t * P, PW + (t + 1) * P)
                    parts = [(v, k, c) for k in range(2) for v, c in ((v_head, 0), (v_head, 1), (v_tail, 0))]
                    for n, (v, k, c) in enumerate(parts):
                        last = nc.tensor.matmul(lg[:, t, :, :, :], v[:, k, at], cw_pts[:, k, c, :, :],
                                                start=n == 0, stop=n == len(parts) - 1)
                last.then_inc(logit_done, 1)

            def point(b, j, t, dst, fresh, first=False):
                at = t * P
                if first:
                    pe.wait_ge(w_heads, j + 1)
                for r in range(K):
                    nc.tensor.matmul(dst, op[b][:, 0, j, at + r * PW:at + r * PW + P], w_head[:, j, r, :],
                                     start=fresh and r == 0, stop=False, skip_group_check=True)
                if first:
                    pe.wait_ge(w_tails, 3 * j + 1)
                nc.tensor.matmul(dst, op[b][:, 0, j, at + 2 * PW:at + 2 * PW + P], w_tail2[:, j, :],
                                 start=False, stop=False, skip_group_check=True)
                if first:
                    pe.wait_ge(w_tails, 3 * j + 3)
                return nc.tensor.matmul(dst, op[b][:, 1, j, at:at + P], w_tail01[:, j, :],
                                        start=False, stop=True, skip_group_check=True)

            def first_point(i, a, n, first=False):
                b, t = i // TPI, i % TPI
                pe.wait_ge(prod_done, n * 2 * TILES + 2 * i + a + 1)
                point(b, a, t, bank[2 * (i % SETS_OF_BANKS) + a][:, :], True, first).then_inc((m1_done, m2_done)[a], 1)

            def first_points(i, n):
                if i % TPI == 0:
                    pe.wait_ge(ops_in[i // TPI][0], (n + 1) * 16 * F_PARTS)
                for a in range(2):
                    first_point(i, a, n)

            def last_points(i, n):
                b, t, s = i // TPI, i % TPI, i % SETS_OF_BANKS
                if t == 0:
                    pe.wait_ge(ops_in[b][1], (n + 1) * 16 * F_PARTS)
                for a in range(2):
                    pe.wait_ge(seeded, n * 2 * TILES + 2 * i + a + 1 + 2 * LOOK)
                    point(b, 2 + a, t, bank[2 * s + a][:, :], False, i == 0).then_inc(y_done, 1)

            def round_(n, more):
                for i in range(TILES):
                    last_points(i, n)
                    if 0 < i < TILES - 2:
                        first_points(i + 2, n)
                    elif i >= TILES - 2 and more:
                        first_points(i + 2 - TILES, n + 1)
                    if more and i == 4:
                        group_sums(n + 1)
                    if more and i == 13:
                        logits(n + 1)
                if more:
                    first_points(2, n + 1)

            pe.wait_ge(mats_loaded, 16)
            group_sums(0)
            pe.wait_ge(ready, 1)
            pe.wait_ge(w_chain, 4)
            for k in range(2):
                last = nc.tensor.matmul(w_bank[0:1, k * P:(k + 1) * P], w_pow2[:, k:k + 1], ident[:, :], start=True, stop=True)
            last.then_inc(w_col, 1)
            pe.wait_ge(w_chain, 5)
            nc.tensor.matmul(w_bank[:, 2 * P:2 * P + 2], ones[0:1, :], w_top[0:1, :], start=True, stop=True).then_inc(w_cast, 1)
            pe.wait_ge(h_done, 1)
            pe.wait_ge(w_chain, 6)
            for k in range(WARM):
                nc.tensor.matmul(w_bank[:, :], v_head[:, 0, 0:P], v_head[:, 0, 0:N], start=True, stop=True)
            pe.wait_ge(c_tails, 1)
            logits(0)
            pe.wait_ge(ops_in[0][0], 16 * F_PARTS)
            for a in range(2):
                for i in range(2):
                    first_point(i, a, 0, i == 0)
            first_points(2, 0)
            with pe.Fori(0, ROUNDS - 1) as n:
                round_(n, True)
            round_(ROUNDS - 1, False)

        @block.scalar
        def _(act):
            def input_heads(m, k, first=False):
                if first and k >= 2:
                    act.wait_ge(late_points, k - 1)
                else:
                    act.wait_ge(v_done, v_count(m, k + 1))
                if k >= 2:
                    v_rows = v_pts[:, k, :].rearrange("p (h w) -> p h w", w=PW)
                    x_rows = x_norm[:, :].rearrange("p (h w a) -> p h w a", w=PW, a=2)
                    col, a = ((0, 1), (PW - 1, 0))[k - 2]
                    act.activation(v_rows[:, :, col:col + 1], x_rows[:, :, col:col + 1, a], ACT.Copy, scale=-1.0) \
                        .then_inc(edge_done, 1)
                    act.wait_ge(edge_done, m * 2 + k - 1)
                if not first:
                    for b in range(2):
                        act.wait_ge(ops_in[b][k // 2], m * 16 * F_PARTS)
                    act.wait_ge(logit_done, m)
                act.activation(v_head[:, k, PW:PW + PAIRS], v_pts[:, k, :], ACT.Copy).then_inc(h_done, 1)

            def exponentials(m):
                act.wait_ge(prep, m * PREP_CHAIN + 9)
                act.activation(mix[:, :, :], logit[:, :, :], ACT.Exp).then_inc(exp_done, 1)

            def round_(n, more):
                for i in range(TILES):
                    act.wait_ge(m1_done, n * TILES + i + 1)
                    act.wait_ge(seeded, n * 2 * TILES + 2 * i + 2)
                    act.activation(m1_sb[:, i % LOOK, :], bank[2 * (i % SETS_OF_BANKS)][:, :], ACT.Copy) \
                        .then_inc(m1_copied, 1)
                    if more and i == 2:
                        act.wait_ge(norm_done, n + 1)
                        for k in range(LOADS):
                            act.dma_start(*x_part(n + 1, k)).then_inc(x_loaded[k], 16)
                    if more and 10 <= i < 10 + NP:
                        input_heads(n + 1, i - 10)
                    if more and i == 16:
                        exponentials(n + 1)

            def w_heads_of(k):
                if k == 0:
                    act.wait_ge(w_point1, K)
                if k == 1:
                    act.wait_ge(w_point2, 1)
                src = w_pts[:, k, :, :] if k < 2 else w_raw[:, :, 2 * (k - 2), :]
                act.activation(w_head[:, k, :, :], src, ACT.Copy,
                               scale=half_scale[:, 0:1] if k < 2 else scale[:, 0:1]).then_inc(w_heads, 1)

            act.dma_start(bias_all[:, :], bias.partition_broadcast(P)).then_inc(small_loaded, 16)
            act.dma_start(cb_all[:, :], coupler_b.partition_broadcast(P)).then_inc(small_loaded, 16)
            act.wait_ge(cleared, 1)
            for b in range(2):
                act.dma_start(cw_pair[C * b:C * b + C, b, :], coupler_w).then_inc(small_loaded, 16)
            act.wait_ge(ready, 1)
            act.activation(ones_exp[:, :], ones[0:1, 0:1], ACT.Exp)
            for r in range(K):
                if r == K - 1:
                    input_heads(0, 0, True)
                act.wait_ge(w_loaded[r], 16 * 2)
                if r:
                    act.wait_ge(w_bounds, r)
                act.activation(w_pts[:, 1, :, :], w_raw[:, r, :, :], ACT.Abs, accum_out=w_max_part[:, r:r + 1]) \
                    .then_inc(w_bounds, 1)
            input_heads(0, 1, True)
            act.wait_ge(w_chain, W_STEPS)
            w_heads_of(0)
            w_heads_of(1)
            input_heads(0, 2, True)
            input_heads(0, 3, True)
            w_heads_of(2)
            w_heads_of(3)
            exponentials(0)
            with act.Fori(0, ROUNDS - 1) as n:
                round_(n, True)
            round_(ROUNDS - 1, False)

        @block.vector
        def _(dve):
            def statistics(m):
                for k in range(CHUNKS):
                    if k % (CHUNKS // LOADS) == 0:
                        dve.wait_ge(x_loaded[k // (CHUNKS // LOADS)], (m + 1) * 16)
                    last = dve.bn_stats(stats[:, k, :], x_raw[:, k * CHUNK:(k + 1) * CHUNK])
                last.then_inc(prep, 1)

            def aggregate(m):
                dve.wait_ge(prep, m * PREP_CHAIN + 1)
                dve.nop(nofuse=True)
                dve.bn_aggr(mean_var[:, :], stats[:, :, :]).then_inc(prep, 1)

            def group_variance(m):
                dve.wait_ge(group_done, m + 1)
                dve.tensor_copy(group[:, :], group_ps).then_inc(prep, 1)
                dve.wait_ge(prep, m * PREP_CHAIN + 3)
                dve.tensor_tensor(diff_sq[:, :], group[:, 2:3], group[:, 2:3], ALU.mult).then_inc(prep, 1)
                dve.wait_ge(prep, m * PREP_CHAIN + 4)
                dve.scalar_tensor_tensor(var_eps[:, :], group[:, 1:2], EPS, diff_sq[:, :], ALU.add, ALU.add).then_inc(prep, 1)

            def normalise(m, first=False):
                dve.wait_ge(rstd_done, m + 1)
                dve.tensor_scalar(norm_scale[:, :], rstd[:, :], X_SCALE, None, ALU.mult).then_inc(prep, 1)
                dve.wait_ge(prep, m * PREP_CHAIN + 6)
                if not first:
                    dve.wait_ge(v_done, v_count(m, 0))
                    dve.wait_ge(edge_done, m * 2)
                dve.tensor_scalar(x_norm[:, :], x_raw[:, :], group[:, 0:1], norm_scale[:, 0:1],
                                  ALU.subtract, ALU.mult).then_inc(norm_done, 1)

            def input_point(m, k, first=False):
                dve.wait_ge(norm_done, m + 1)
                if not first:
                    dve.wait_ge(t_done, m * NP - NP + k + 1)
                v_out, left, right = point_operands(k)
                dve.tensor_tensor(v_out, left, right, ALU.add if k == 0 else ALU.subtract).then_inc(v_done, 1)

            def with_bias(m):
                dve.wait_ge(logit_done, m + 1)
                dve.scalar_tensor_tensor(logit[:, :, :], logit_ps.rearrange("p (q s) -> p q s", s=SETS), undo[:, 1:2],
                                         cb_all[:, :].unsqueeze(1).to_broadcast([P, PIX, SETS]), ALU.mult, ALU.add) \
                    .then_inc(prep, 1)

            def maximum(m):
                dve.wait_ge(prep, m * PREP_CHAIN + 7)
                dve.tensor_reduce(top[:, :], logit[:, :, :], axis=AX.X, op=ALU.max).then_inc(prep, 1)

            def less_maximum(m):
                dve.wait_ge(prep, m * PREP_CHAIN + 8)
                dve.tensor_tensor(logit[:, :, :], logit[:, :, :], spread(top[:, :], SETS), ALU.subtract).then_inc(prep, 1)

            def add_up(m):
                dve.wait_ge(exp_done, m + 1)
                dve.tensor_reduce(total[:, :], mix[:, :, :], axis=AX.X, op=ALU.add).then_inc(prep, 1)

            def invert(m):
                dve.wait_ge(prep, m * PREP_CHAIN + 10)
                dve.reciprocal(total[:, :], total[:, :]).then_inc(prep, 1)

            def divide(m):
                dve.wait_ge(prep, m * PREP_CHAIN + 11)
                dve.tensor_tensor(logit[:, :, :], mix[:, :, :], spread(total[:, :], SETS), ALU.mult).then_inc(prep, 1)

            def add_up_again(m):
                dve.wait_ge(prep, m * PREP_CHAIN + 12)
                dve.tensor_reduce(top[:, :], logit[:, :, :], axis=AX.X, op=ALU.add).then_inc(prep, 1)

            def invert_again(m):
                dve.wait_ge(prep, m * PREP_CHAIN + 13)
                dve.reciprocal(top[:, :], top[:, :]).then_inc(prep, 1)

            def divide_again(m):
                dve.wait_ge(prep, m * PREP_CHAIN + 14)
                dve.tensor_tensor(mix[:, :, :], logit[:, :, :], spread(top[:, :], SETS), ALU.mult).then_inc(prep, 1)

            def selection(m, dst, signal):
                dve.wait_ge(prep, m * PREP_CHAIN + 15)
                dve.tensor_reduce(dst[1], mix[:, :, :], axis=AX.X, op=ALU.add).then_inc(prep, 1)
                dve.tensor_scalar(dst[0], mix[:, :, :], undo[:, 0:1], None, ALU.mult).then_inc(signal, 1)

            def seed(i, n, pixels=(0, 1)):
                plus, minus = (bank[2 * (i % SETS_OF_BANKS) + a] for a in range(2))
                m1 = m1_sb[:, i % LOOK, :]
                if 0 in pixels:
                    dve.wait_ge(m2_done, n * TILES + i + 1)
                    dve.wait_ge(m1_copied, n * TILES + i + 1)
                    dve.tensor_tensor(plus[:, :], minus[:, :], m1, ALU.add).then_inc(seeded, 1)
                if 1 in pixels:
                    dve.tensor_tensor(minus[:, :], m1, minus[:, :], ALU.subtract).then_inc(seeded, 1)

            def multiply(i, n):
                for a in range(2):
                    dve.wait_ge(half_done, n * 2 * TILES + 2 * i + a + 1)
                    dve.wait_ge(y_done, n * 2 * TILES + 2 * i + a + 1)
                    dve.tensor_tensor(prod[:, a, :, :],
                                      bank[2 * (i % SETS_OF_BANKS) + a][:, :].rearrange("p (s c) -> p s c", c=C),
                                      spread(sel_w[:, 2 * i + a, :], C), ALU.mult).then_inc(prod_done, 1)

            def halve(i, n):
                dve.wait_ge(half_used, n * TILES + i + 1)
                for a in range(2):
                    dve.wait_ge(prod_done, n * 2 * TILES + 2 * i + a + 1 + 2 * SETS_OF_BANKS)
                    dve.tensor_tensor(half[:, i % LOOK, a, :, :], prod[:, a, 0:SETS // 2, :],
                                      prod[:, a, SETS // 2:SETS, :], ALU.add).then_inc(half_done, 1)

            def last_tile(n):
                i = TILES - 1
                b, t = i // TPI, i % TPI
                hf = half[:, i % LOOK, :, :, :]
                dve.wait_ge(half_used, n * TILES + i + 1)
                dve.wait_ge(xb_done, n * 2 + b + 1)
                dve.wait_ge(stored[b], n * 16 + 16)
                def product(a):
                    done = n * 2 * TILES + 2 * i + a + 1
                    dve.wait_ge(half_done, done)
                    dve.wait_ge(y_done, done)
                    dve.tensor_tensor(prod[:, a, :, :],
                                      bank[2 * (i % SETS_OF_BANKS) + a][:, :].rearrange("p (s c) -> p s c", c=C),
                                      spread(sel_w[:, 2 * i + a, :], C), ALU.mult).then_inc(prod_done, 1)

                def to_four(a):
                    dve.wait_ge(prod_done, n * 2 * TILES + 2 * i + a + 1 + 2 * SETS_OF_BANKS)
                    dve.tensor_tensor(hf[:, a, :, :], prod[:, a, 0:SETS // 2, :],
                                      prod[:, a, SETS // 2:SETS, :], ALU.add).then_inc(half_done, 1)

                def to_two(a):
                    dve.wait_ge(half_done, n * 2 * TILES + 2 * i + a + 1 + 2)
                    dve.tensor_tensor(last_quarter[:, a, :, :], hf[:, a, 0:2, :], hf[:, a, 2:4, :], ALU.add) \
                        .then_inc(last_steps[a], 1)

                def to_one(a):
                    dve.wait_ge(last_steps[a], 1)
                    dve.tensor_tensor(last_mixed[:, a, :], last_quarter[:, a, 0, :], last_quarter[:, a, 1, :], ALU.add) \
                        .then_inc(last_steps[a], 1)

                def result(a):
                    dve.wait_ge(last_steps[a], 2)
                    dve.tensor_tensor(y_out[b][:, t, a, :], last_mixed[:, a, :], x_res[b][:, t, a, :], ALU.add) \
                        .then_inc(last_steps[a], 1)

                product(0)
                to_four(0)
                product(1)
                to_two(0)
                to_four(1)
                to_one(0)
                to_two(1)
                result(0)
                to_one(1)
                result(1)

            def take_selection(n):
                dve.wait_ge(sel_done, n)
                dve.wait_ge(prod_done, n * 2 * TILES + 2 * SETS_OF_BANKS)
                dve.wait_ge(xb_done, n * 2)
                dve.tensor_copy(sel_now[:, :], sel_next[:, :]).then_inc(sel_copied, 1)

            def round_(n, more):
                for i in range(TILES):
                    if i == 0:
                        dve.wait_ge(sel_copied, n + 1)
                    if i + 1 < TILES or more:
                        multiply(i, n)
                        halve(i, n)
                    else:
                        last_tile(n)
                    if i + 2 < TILES:
                        seed(i + 2, n)
                    elif more:
                        seed(i + 2 - TILES, n + 1)
                    if more and i == 2:
                        statistics(n + 1)
                        aggregate(n + 1)
                    if more and i == 5:
                        group_variance(n + 1)
                    if more and i == 7:
                        normalise(n + 1)
                    if more and 8 <= i < 8 + NP:
                        input_point(n + 1, i - 8)
                    if more and i == 14:
                        with_bias(n + 1)
                        maximum(n + 1)
                        less_maximum(n + 1)
                    if more and i == 15:
                        add_up(n + 1)
                        invert(n + 1)
                        divide(n + 1)
                    if more and i == 16:
                        add_up_again(n + 1)
                        invert_again(n + 1)
                        divide_again(n + 1)
                        selection(n + 1, sel_next_parts, sel_done)
                if more:
                    take_selection(n + 1)

            dve.memset(diff_sq[:, :], 0.0).then_inc(seeded, 2 * LOOK)
            dve.memset(var_eps[:, :], 0.0).then_inc(prod_done, 2 * SETS_OF_BANKS)
            dve.memset(norm_scale[:, :], 0.0).then_inc(half_done, 2)
            def w_tails_of(k, parts=(0, 1, 2)):
                src = w_pts[:, k, :, :] if k < 2 else w_raw[:, :, 2 * (k - 2), :]
                for part in parts:
                    if part == 0:
                        dve.wait_ge(w_heads, k + 1)
                    lo, hi, r, tail = ((0, P, 2, w_tail2), (0, C, 0, w_tail01), (C, P, 1, w_tail01))[part]
                    by = half_scale[lo:hi, 0:1] if k < 2 else scale[lo:hi, 0:1]
                    dve.scalar_tensor_tensor(tail[lo:hi, k, :], src[lo:hi, r, :], by, w_head[lo:hi, k, r, :],
                                             ALU.mult, ALU.subtract).then_inc(w_tails, 1)

            def coupler_parts():
                cw = cw_pair[:, :, :].rearrange("p b s -> p (b s)")
                parts = ((0, 0, half_scale), (0, 1, half_scale), (1, 0, minus_half_scale), (1, 1, half_scale))
                dve.wait_ge(w_chain, W_STEPS)
                for k, a, by in parts:
                    last = dve.tensor_scalar(cw_pts[:, k, 0, a, :], cw, by[:, 1:2], None, ALU.mult)
                last.then_inc(c_heads, 1)
                dve.wait_ge(c_heads, 1)
                for k, a, by in parts:
                    last = dve.scalar_tensor_tensor(cw_pts[:, k, 1, a, :], cw, by[:, 1:2], cw_pts[:, k, 0, a, :],
                                                    ALU.mult, ALU.subtract)
                last.then_inc(c_tails, 1)

            def input_tails_of(k):
                dve.wait_ge(h_done, k + 1)
                dve.tensor_tensor(v_tail[:, k, PW:PW + PAIRS], v_pts[:, k, :], v_head[:, k, PW:PW + PAIRS],
                                  ALU.subtract).then_inc(t_done, 1)

            statistics(0)
            aggregate(0)
            group_variance(0)
            dve.wait_ge(small_loaded, 16 * 4)
            dve.tensor_reduce(w_max[:, 1:2], cw_pair[:, :, :].rearrange("p b s -> p (b s)"), axis=AX.X, op=ALU.max,
                              apply_absolute_value=True).then_inc(w_chain, 1)
            normalise(0, True)
            for k in range(2):
                input_point(0, k, True)
            dve.wait_ge(ready, 1)
            input_tails_of(0)
            dve.wait_ge(w_bounds, K)
            dve.tensor_reduce(w_max[:, 0:1], w_max_part[:, :], axis=AX.X, op=ALU.max).then_inc(w_chain, 1)
            dve.wait_ge(w_chain, 2)
            dve.tensor_scalar(w_max[:, :], w_max[:, :], TINY, None, ALU.max).then_inc(w_chain, 1)
            dve.wait_ge(w_chain, 3)
            dve.tensor_scalar(w_pow2[:, :].bitcast(I32), w_max[:, :].bitcast(I32), 0x7F800000, None,
                              ALU.bitwise_and).then_inc(w_chain, 1)

            dve.wait_ge(w_sums, K)
            dve.tensor_tensor(w_pts[:, 1, :, :], w_sum[:, :, :], w_raw[:, :, 1, :], ALU.subtract).then_inc(w_point2, 1)
            dve.wait_ge(w_col, 1)
            dve.tensor_reduce(w_top[0:1, :], w_bank[0:1, 0:2 * P].rearrange("p (k q) -> p k q", k=2), axis=AX.X,
                              op=ALU.max).then_inc(w_chain, 1)
            input_tails_of(1)
            dve.wait_ge(w_cast, 1)
            dve.tensor_copy(magnitude[:, :], w_bank[:, 2 * P:2 * P + 2]).then_inc(w_chain, 1)
            dve.wait_ge(w_chain, 6)
            dve.reciprocal(inverse[:, :], magnitude[:, :]).then_inc(w_chain, 1)
            dve.tensor_scalar(undo[:, :], magnitude[:, :], 1.0 / (W_TOP * X_SCALE), None, ALU.mult).then_inc(w_chain, 1)
            dve.wait_ge(w_chain, 7)
            for dst, by in ((half_scale, W_TOP / 2), (minus_half_scale, -W_TOP / 2), (scale, W_TOP)):
                dve.tensor_scalar(dst[:, :], inverse[:, :], by, None, ALU.mult).then_inc(w_chain, 1)
            coupler_parts()
            w_tails_of(0)
            w_tails_of(1)
            with_bias(0)
            maximum(0)
            less_maximum(0)
            w_tails_of(2)
            w_tails_of(3, (0,))
            seed(0, 0)
            add_up(0)
            w_tails_of(3, (1,))
            invert(0)
            w_tails_of(3, (2,))
            divide(0)
            seed(1, 0, (0,))
            add_up_again(0)
            seed(1, 0, (1,))
            invert_again(0)
            divide_again(0)
            selection(0, sel_now_parts, sel_copied)
            with dve.Fori(0, ROUNDS - 1) as n:
                round_(n, True)
            round_(ROUNDS - 1, False)

        @block.gpsimd
        def _(pool):
            def inverse_deviation(m):
                pool.wait_ge(prep, m * PREP_CHAIN + 5)
                pool.tensor_tensor(rstd[:, :], var_eps[:, :], minus_half[:, :], ALU.pow).then_inc(rstd_done, 1)

            def input_tails(m, k, first=False):
                pool.wait_ge(h_done, m * NP + k + 1)
                if first:
                    pool.wait_ge(t_done, k)
                for b in range(0 if first else 2):
                    pool.wait_ge(ops_in[b][k // 2], m * 16 * F_PARTS)
                if not first:
                    pool.wait_ge(logit_done, m)
                pool.tensor_tensor(v_tail[:, k, PW:PW + PAIRS], v_pts[:, k, :], v_head[:, k, PW:PW + PAIRS],
                                   ALU.subtract).then_inc(t_done, 1)

            def input_and_bias(b, n):
                pool.wait_ge(sel_copied, n + 1)
                q0 = b * TPI * 2
                pool.tensor_tensor(bias_part[:, :, :], bias_all[:, :].unsqueeze(1).to_broadcast([P, TPI * 2, C]),
                                   spread(sel_sum[:, q0:q0 + TPI * 2], C), ALU.mult).then_inc(bias_done, 1)
                pool.wait_ge(xres_in[b], (n + 1) * 16)
                pool.wait_ge(bias_done, n * 2 + b + 1)
                xr = x_res[b][:, :, :, :].rearrange("p t a c -> p (t a) c")
                pool.tensor_tensor(xr, xr, bias_part[:, :, :], ALU.add).then_inc(xb_done, 1)

            def finish(i, n):
                b, t = i // TPI, i % TPI
                pool.wait_ge(half_done, n * 2 * TILES + 2 * i + 2 + 2)
                hf = half[:, i % LOOK, :, :, :]
                pool.tensor_tensor(quarter[:, :, :, :].rearrange("p a s c -> p a (s c)"),
                                   hf[:, :, 0:2, :].rearrange("p a s c -> p a (s c)"),
                                   hf[:, :, 2:4, :].rearrange("p a s c -> p a (s c)"), ALU.add).then_inc(half_used, 1)
                pool.wait_ge(half_used, n * TILES + i + 1 + LOOK)
                pool.tensor_tensor(mixed[:, :, :], quarter[:, :, 0, :], quarter[:, :, 1, :], ALU.add).then_inc(mixed_done, 1)
                pool.wait_ge(mixed_done, n * TILES + i + 1)
                if t == 0:
                    pool.wait_ge(xb_done, n * 2 + b + 1)
                    pool.wait_ge(stored[b], n * 16 + 16)
                pool.tensor_tensor(y_out[b][:, t, :, :], mixed[:, :, :], x_res[b][:, t, :, :], ALU.add).then_inc(out_done, 1)

            def round_(n, more):
                for i in range(TILES):
                    if i % TPI == 0:
                        input_and_bias(i // TPI, n)
                    if i + 1 < TILES or more:
                        finish(i, n)
                    if more and i == 4:
                        inverse_deviation(n + 1)
                    if more and 9 <= i < 9 + NP:
                        input_tails(n + 1, i - 9)

            pool.memset(cw_pair[:, :, :], 0.0).then_inc(cleared, 1)
            pool.memset(minus_half[:, :], -0.5)
            pool.memset(ones[:, :], 1.0)
            for edge in (0, PW + PAIRS):
                pool.memset(v_head[:, :, edge:edge + PW], 0.0)
                last = pool.memset(v_tail[:, :, edge:edge + PW], 0.0)
            last.then_inc(ready, 1)
            pool.wait_ge(ready, 1)
            pool.memset(quarter[:, 0, 0, 0:1], 0.0).then_inc(half_used, LOOK)
            pool.memset(mixed[:, 0, 0:1], 0.0).then_inc(out_done, 1)
            for b in range(2):
                pool.memset(y_out[b][:, 0, 0, 0:1], 0.0).then_inc(stored[b], 16)

            def kernel_sum(r):
                pool.wait_ge(w_loaded[r], 16 * 2)
                pool.tensor_tensor(w_sum[:, r, :], w_raw[:, r, 0, :], w_raw[:, r, 2, :], ALU.add).then_inc(w_sums, 1)

            def kernel_point1(r):
                pool.wait_ge(w_sums, r + 1)
                pool.tensor_tensor(w_pts[:, 0, r, :], w_sum[:, r, :], w_raw[:, r, 1, :], ALU.add).then_inc(w_point1, 1)

            inverse_deviation(0)
            kernel_sum(0)
            kernel_sum(1)
            kernel_point1(0)
            kernel_sum(2)
            kernel_point1(1)
            kernel_point1(2)

            def late_point(k):
                pool.wait_ge(norm_done, 1)
                v_out, left, right = point_operands(k)
                pool.tensor_tensor(v_out, left, right, ALU.subtract).then_inc(late_points, 1)

            for k in range(2, NP):
                late_point(k)
            for k in range(2, NP):
                input_tails(0, k, True)
            pool.wait_ge(small_loaded, 16 * 4)
            with pool.Fori(0, ROUNDS - 1) as n:
                round_(n, True)
            round_(ROUNDS - 1, False)


def kernel(x, L0_conv_coupler_w, L0_conv_coupler_b, L0_conv_weight, L0_conv_bias):
    import numpy as np
    import concourse.bacc as bacc
    from concourse.bass_utils import run_bass_kernel_spmd

    x = np.asarray(x)
    x_pix = x.transpose(0, 2, 3, 1).reshape(IMAGES, TPI, P, 2 * C)
    weight = np.asarray(L0_conv_weight).transpose(1, 3, 4, 2, 0).reshape(C, K, K * N)
    same_group = np.kron(np.eye(P // 2, dtype=np.float32), np.ones((2, 2), np.float32))
    eye = np.eye(P, dtype=np.float32)
    matrices = np.stack([0.5 * same_group, eye - 0.5 * same_group, eye], axis=1)

    host = {
        "x": x,
        "x_pix": x_pix,
        "weight": weight,
        "bias": np.asarray(L0_conv_bias),
        "coupler_w": np.asarray(L0_conv_coupler_w).reshape(SETS, C).T,
        "coupler_b": np.asarray(L0_conv_coupler_b),
        "matrices": matrices,
    }
    host = {name: np.ascontiguousarray(a) for name, a in host.items()}
    nc = bacc.Bacc("TRN2", target_bir_lowering=False, num_devices=1)
    args = {name: nc.dram_tensor(name, a.shape, F32, kind="ExternalInput").ap() for name, a in host.items()}
    out = nc.dram_tensor("out", x_pix.shape, F32, kind="ExternalOutput").ap()
    program(nc, out=out, **args)
    got = run_bass_kernel_spmd(nc, [host], core_ids=[0]).results[0]["out"]
    return got.reshape(IMAGES, H, W, C).transpose(0, 3, 1, 2)
```
